# Optimizing a Trainium2 kernel written in Bass

```python
import numpy as np
import jax
import jax.numpy as jnp

def _softmax(x, axis=-1):
    return jax.nn.softmax(x, axis=axis)

def _gelu(x):
    return jax.nn.gelu(x, approximate=True)

def _silu(x):
    return jax.nn.silu(x)

def _sigmoid(x):
    return jax.nn.sigmoid(x)

def _layernorm(x, axis=-1, eps=1e-05):
    m = jnp.mean(x, axis=axis, keepdims=True)
    v = jnp.var(x, axis=axis, keepdims=True)
    return (x - m) / jnp.sqrt(v + eps)

def _scatter_add(tgt, idx, src, axis=0):
    return tgt.at[idx].add(src)

def _segment_sum(src, seg, n):
    return jax.ops.segment_sum(src, seg, n)
kernel_name = 'mk_flamingo_gated_d1_seqx_r4_93865a'

def setup_inputs(seed: int=0):
    np.random.seed(seed)
    _w = jnp.asarray

    def _rec_inputs():
        import jax
        import jax.numpy as jnp
        _rk = jax.random.key(seed)
        x = 7.22e-05 + 1 * jax.random.normal(jax.random.fold_in(_rk, 1), (8, 112, 256), jnp.float32)
        _lenS = 112 - jax.random.randint(jax.random.fold_in(_rk, 7), (8,), 0, max(1, 112 // 4) + 1, jnp.int32)
        _lenS2 = 375 - jax.random.randint(jax.random.fold_in(_rk, 8), (8,), 0, max(1, 375 // 4) + 1, jnp.int32)
        _ctx_1024P = jax.random.normal(jax.random.fold_in(_rk, 11), (8, 16, 256), jnp.float32)
        _ctx_1024c = jax.random.dirichlet(jax.random.fold_in(_rk, 511), 0.3 * jnp.ones((16,), jnp.float32), (8, 375))
        _ctx_1024t = jnp.einsum('bsk,bkd->bsd', _ctx_1024c, _ctx_1024P)
        _ctx_1024t = _ctx_1024t * jax.lax.rsqrt(jnp.mean(jnp.square(_ctx_1024t)) + 1e-12) * 0.953939
        ctx_1024 = 4.13588e-05 + 0.999923 * (_ctx_1024t + 0.3 * jax.random.normal(jax.random.fold_in(_rk, 611), (8, 375, 256), jnp.float32))
        _validS = jnp.arange(112)[None, :] < _lenS[:, None]
        _validS2 = jnp.arange(375)[None, :] < _lenS2[:, None]
        _causal = jnp.tril(jnp.ones((112, 112), dtype=bool))
        mask_Bx1xSxS2_bk1 = jnp.broadcast_to(_validS2[:, None, None, :], (8, 1, 112, 375))
        _g = jax.random.normal(jax.random.fold_in(_rk, 9001), (2, 1), jnp.float32)
        _g = jnp.sign(_g) * jnp.maximum(jnp.abs(_g), 1.0) + (_g == 0) * 1.0
        g_xattn = _g[0]
        g_ffn = _g[1]
        return (x, ctx_1024, mask_Bx1xSxS2_bk1, g_xattn, g_ffn)
    x, ctx_1024, mask_Bx1xSxS2_bk1, g_xattn, g_ffn = _rec_inputs()

    def _L0_xattn_setup():
        import jax, jax.numpy as jnp
        import numpy as np
        B, S, D, H = (4, 512, 256, 16)
        HD = D // H
        key = jax.random.key(seed)
        ks = jax.random.split(key, 12)
        scale = 1.0 / np.sqrt(D)
        inp = {'queries': jax.random.normal(ks[0], (B, S, D), jnp.float32), 'keys': jax.random.normal(ks[1], (B, S, D), jnp.float32), 'values': jax.random.normal(ks[2], (B, S, D), jnp.float32), 'mask': jax.random.randint(ks[3], (B, 1, S, S), 0, 2).astype(bool), 'Wq': jax.random.normal(ks[4], (D, D), jnp.float32) * scale, 'bq': jnp.zeros((D,), jnp.float32), 'Wk': jax.random.normal(ks[5], (D, D), jnp.float32) * scale, 'bk': jnp.zeros((D,), jnp.float32), 'Wv': jax.random.normal(ks[6], (D, D), jnp.float32) * scale, 'bv': jnp.zeros((D,), jnp.float32), 'Wo': jax.random.normal(ks[7], (D, D), jnp.float32) * scale, 'bo': jnp.zeros((D,), jnp.float32)}
        return inp
    _L0_xattn_all = _L0_xattn_setup()
    _L0_xattn_in = {k: v for k, v in _L0_xattn_all.items() if k in ('Wq', 'bq', 'Wk', 'bk', 'Wv', 'bv', 'Wo', 'bo')}
    del _L0_xattn_all

    def _L0_ffn_setup():
        import jax, jax.numpy as jnp
        import numpy as np
        D_MODEL = 256
        D_FF = 1024
        N_ZONES = 8
        TOP_K = 3
        ROUTER_H = 64
        BATCH = 16
        SEQ = 512
        key = jax.random.key(seed)
        ks = jax.random.split(key, 8)
        s = lambda *dims: 1.0 / np.sqrt(dims[-2] if len(dims) > 1 else dims[-1])
        x = jax.random.normal(ks[0], (BATCH, SEQ, D_MODEL), dtype=jnp.float32)
        W1 = jax.random.normal(ks[1], (D_MODEL, ROUTER_H), dtype=jnp.float32) / np.sqrt(D_MODEL)
        b1 = jnp.zeros((ROUTER_H,), dtype=jnp.float32)
        W2 = jax.random.normal(ks[2], (ROUTER_H, N_ZONES), dtype=jnp.float32) / np.sqrt(ROUTER_H)
        b2 = jnp.zeros((N_ZONES,), dtype=jnp.float32)
        Wa = jax.random.normal(ks[3], (N_ZONES, D_MODEL, D_FF), dtype=jnp.float32) / np.sqrt(D_MODEL)
        Wb = jax.random.normal(ks[4], (N_ZONES, D_FF, D_MODEL), dtype=jnp.float32) / np.sqrt(D_FF)
        return {'x': x, 'W1': W1, 'b1': b1, 'W2': W2, 'b2': b2, 'Wa': Wa, 'Wb': Wb}
    _L0_ffn_all = _L0_ffn_setup()
    _L0_ffn_in = {k: v for k, v in _L0_ffn_all.items() if k in ('W1', 'b1', 'W2', 'b2', 'Wa', 'Wb')}
    del _L0_ffn_all
    return {'x': x, 'ctx_1024': ctx_1024, 'mask_Bx1xSxS2_bk1': mask_Bx1xSxS2_bk1, 'g_xattn': g_xattn, 'g_ffn': g_ffn, 'L0_xattn_Wq': _L0_xattn_in['Wq'], 'L0_xattn_bq': _L0_xattn_in['bq'], 'L0_xattn_Wk': _L0_xattn_in['Wk'], 'L0_xattn_bk': _L0_xattn_in['bk'], 'L0_xattn_Wv': _L0_xattn_in['Wv'], 'L0_xattn_bv': _L0_xattn_in['bv'], 'L0_xattn_Wo': _L0_xattn_in['Wo'], 'L0_xattn_bo': _L0_xattn_in['bo'], 'L0_ffn_W1': _L0_ffn_in['W1'], 'L0_ffn_b1': _L0_ffn_in['b1'], 'L0_ffn_W2': _L0_ffn_in['W2'], 'L0_ffn_b2': _L0_ffn_in['b2'], 'L0_ffn_Wa': _L0_ffn_in['Wa'], 'L0_ffn_Wb': _L0_ffn_in['Wb']}

def reference(x, ctx_1024, mask_Bx1xSxS2_bk1, g_xattn, g_ffn, L0_xattn_Wq, L0_xattn_bq, L0_xattn_Wk, L0_xattn_bk, L0_xattn_Wv, L0_xattn_bv, L0_xattn_Wo, L0_xattn_bo, L0_ffn_W1, L0_ffn_b1, L0_ffn_W2, L0_ffn_b2, L0_ffn_Wa, L0_ffn_Wb):
    import jax
    import jax.numpy as jnp

    def _L0_xattn_ref(queries, keys, values, mask, Wq, bq, Wk, bk, Wv, bv, Wo, bo):
        import jax, jax.numpy as jnp
        import numpy as np
        B, S, D, H = (4, 512, 256, 16)
        HD = D // H
        b, sq, d = queries.shape

        def split_heads(x):
            return x.reshape(b, x.shape[1], H, HD).transpose(0, 2, 1, 3)
        q = split_heads(queries @ Wq + bq)
        k = split_heads(keys @ Wk + bk)
        v = split_heads(values @ Wv + bv)
        scores = jnp.einsum('bhqd,bhkd->bhqk', q, k) / jnp.sqrt(jnp.float32(HD))
        scores = jnp.where(mask, jnp.float32(-1000000000000000.0), scores)
        attn = jax.nn.softmax(scores, axis=-1)
        ctx = jnp.einsum('bhqk,bhkd->bhqd', attn, v)
        ctx = ctx.transpose(0, 2, 1, 3).reshape(b, sq, d)
        return ctx @ Wo + bo

    def _L0_ffn_ref(x, W1, b1, W2, b2, Wa, Wb):
        import jax, jax.numpy as jnp
        import numpy as np
        D_MODEL = 256
        D_FF = 1024
        N_ZONES = 8
        TOP_K = 3
        ROUTER_H = 64
        BATCH = 16
        SEQ = 512
        pooled = x.mean(axis=1)
        h = jnp.tanh(pooled @ W1 + b1)
        logits = h @ W2 + b2
        probs = jax.nn.softmax(logits, axis=-1)
        top_p, top_i = jax.lax.top_k(probs, TOP_K)
        top_w = top_p / top_p.sum(axis=-1, keepdims=True)
        onehot = jax.nn.one_hot(top_i, N_ZONES, dtype=x.dtype)
        w = jnp.einsum('bk,bke->be', top_w, onehot)
        zone_outputs = jnp.zeros_like(x)
        for e in range(N_ZONES):
            z = jax.nn.gelu(x @ Wa[e]) @ Wb[e]
            zone_outputs = zone_outputs + z * w[:, e, None, None]
        return x + zone_outputs
    x = x + jnp.tanh(g_xattn[0]) * _L0_xattn_ref(_layernorm(x, axis=-1), ctx_1024, ctx_1024, mask_Bx1xSxS2_bk1, L0_xattn_Wq, L0_xattn_bq, L0_xattn_Wk, L0_xattn_bk, L0_xattn_Wv, L0_xattn_bv, L0_xattn_Wo, L0_xattn_bo)
    x = x + jnp.tanh(g_ffn[0]) * _L0_ffn_ref(_layernorm(x, axis=-1), L0_ffn_W1, L0_ffn_b1, L0_ffn_W2, L0_ffn_b2, L0_ffn_Wa, L0_ffn_Wb)
    return x

_drawn_inputs = setup_inputs


def setup_inputs(seed=0):
    import zlib

    import numpy as np

    out = dict(_drawn_inputs(seed))
    spreads = {'L0_xattn_bq': (0.0, 0.402),
     'L0_xattn_bk': (0.0, 0.8),
     'L0_xattn_bv': (0.0, 0.1),
     'L0_xattn_bo': (0.0, 0.1),
     'L0_ffn_b1': (0.0, 0.1),
     'L0_ffn_b2': (0.0, 0.1)}
    factors = {}
    for name, (base, spread) in spreads.items():
        noise = np.random.default_rng([zlib.crc32(name.encode()), seed]).standard_normal(out[name].shape)
        drawn = base * np.exp(spread * noise) if base else spread * noise
        out[name] = jnp.asarray(drawn.astype(out[name].dtype))
    for name, factor in factors.items():
        out[name] = (out[name] * factor).astype(out[name].dtype)
    return out
```

```python
from contextlib import ExitStack

import concourse.bass as bass
from concourse import mybir

F32 = mybir.dt.float32
F16 = mybir.dt.float16
BF16 = mybir.dt.bfloat16
U8 = mybir.dt.uint8
U32 = mybir.dt.uint32
ALU = mybir.AluOpType
ACT = mybir.ActivationFunctionType
AX = mybir.AxisListType

B, SQ, D, SK = 8, 112, 256, 375
NH, HD = 16, 16
DT = D // 128
KC = 3
CK = SK // KC
PAIRS = NH // 2
FF, NZ, RH, TOPK = 1024, 8, 64, 3
FT = FF // 128
EPS = 1e-5
MASKED = -1e15
WSCALE = 64.0
CHUNK = 1024
CHUNKS = 4
NCH = B * CHUNKS
POST_USES, V_USES, PREP_USES = 3, 2, 6


def uses_before(b):
    full = POST_USES + V_USES + PREP_USES
    if isinstance(b, int) and b == 0:
        return PREP_USES
    return PREP_USES + V_USES + PREP_USES + full * (b - 1)


class Steps:

    def __init__(self, eng, sem):
        self.eng, self.sem, self.base, self.n = eng, sem, 0, 0

    def begin(self, base):
        self.base, self.n = base, 0

    def done(self, ins):
        ins.then_inc(self.sem, 1)
        self.n += 1

    def link(self, ins):
        self.done(ins)
        self.eng.wait_ge(self.sem, self.base + self.n)


def flamingo_layer(nc, x, ctx, mask, g_xattn, g_ffn, Wq, bq, Wk, bk, Wv, bv, Wo, bo,
                   W1, b1, W2, b2, Wa, Wb, out):
    with ExitStack() as stack:
        def sb(name, shape, dt=F32):
            return stack.enter_context(nc.sbuf_tensor(name, shape, dt))

        def sem(name):
            return stack.enter_context(nc.semaphore(name))

        k_scr = nc.dram_tensor("k_scr", [B, 32, 2, PAIRS, SK], F16).ap()
        q_scr = nc.dram_tensor("q_scr", [B, 2, 32, PAIRS, SQ], F16).ap()
        r_scr = nc.dram_tensor("r_scr", [B, SQ, D], F32).ap()
        x2_scr = nc.dram_tensor("x2_scr", [B, 128, 2 * DT * SQ], F16).ap()

        wa = sb("wa", [128, NZ * 2 * DT * FF], F16)
        wb = sb("wb", [128, NZ * 2 * FT * D], F16)
        stage = sb("stage", [128, 2, CHUNK])
        wqkvo = sb("wqkvo", [128, 4, DT, D])
        bq_c = sb("bq_c", [128, DT])
        bk_c = sb("bk_c", [128, DT])
        bv_r = sb("bv_r", [128, D])
        bo_r = sb("bo_r", [128, D])
        w1_s = sb("w1_s", [128, DT, RH])
        w2_s = sb("w2_s", [RH, NZ])
        b1_c = sb("b1_c", [RH, 1])
        b2_r = sb("b2_r", [B, NZ])
        gates = sb("gates", [128, 2])
        tgate = sb("tgate", [128, 2])
        tf_w = sb("tf_w", [128, 1])
        ident = sb("ident", [128, 128])
        ident_b = sb("ident_b", [SQ, SQ], BF16)
        half = sb("half", [128, 1])
        ones = sb("ones", [B, 128])
        ctx_s = sb("ctx_s", [CK, KC, D])
        ctxT = sb("ctxT", [128, DT, SK])
        k_hl = sb("k_hl", [128, DT, 2, SK], F16)
        q_f = sb("q_f", [128, DT * SQ])
        q_hl = sb("q_hl", [128, 2, DT * SQ], F16)
        kst = sb("kst", [128, 2, PAIRS * SK], F16)
        qst = sb("qst", [128, 2, PAIRS, SQ], F16)
        vpad = sb("vpad", [CK, KC, PAIRS, 64])
        probs = sb("probs", [SQ, 2, 2, SK])
        pT = sb("pT", [CK, 2, KC, 2 * SQ])
        mask_s = sb("mask_s", [SQ, SK], U8)
        maskb = sb("maskb", [SQ, 2, SK], BF16)
        xa = sb("xa", [SQ, D])
        xT = sb("xT", [128, DT * SQ])
        xr = sb("xr", [SQ, D])
        yo = sb("yo", [SQ, D])
        x2 = sb("x2", [SQ, D])
        res = sb("res", [SQ, D])
        x2T = sb("x2T", [128, 2, DT * SQ], F16)
        stat = sb("stat", [SQ, 6])
        mv = sb("mv", [SQ, 2])
        ve = sb("ve", [SQ, 1])
        rstd = sb("rstd", [SQ, 1])
        stat2 = sb("stat2", [SQ, 6])
        mv2 = sb("mv2", [SQ, 2])
        ve2 = sb("ve2", [SQ, 1])
        rstd2 = sb("rstd2", [SQ, 1])
        negmax = sb("negmax", [SQ, NH])
        rowsum = sb("rowsum", [SQ, 2, NH])
        rinv = sb("rinv", [SQ, NH])
        rexp = sb("rexp", [SQ, NH, HD])
        rT = sb("rT", [128, DT * SQ])
        oT = sb("oT", [128, DT * SQ])
        pooled = sb("pooled", [128, DT, B])
        h_s = sb("h_s", [RH, B])
        lg = sb("lg", [B, NZ])
        top = sb("top", [B, NZ])
        nmx = sb("nmx", [B, 1])
        ez = sb("ez", [B, NZ])
        zs = sb("zs", [B, 1])
        zr = sb("zr", [B, 1])
        pz = sb("pz", [B, NZ])
        ptop = sb("ptop", [B, NZ])
        pidx = sb("pidx", [B, NZ], U32)
        ts = sb("ts", [B, 1])
        tr = sb("tr", [B, 1])
        wz = sb("wz", [B, TOPK])
        wdiag = sb("wdiag", [B, B, TOPK])
        wbc = sb("wbc", [128, B * TOPK])
        wcur = sb("wcur", [128, 2, TOPK])
        idx_row = sb("idx_row", [1, B * NZ], U32)
        x2b = sb("x2b", [128, 2, 2 * DT * SQ], F16)
        h_f = kst[:].rearrange("p a f -> p (a f)")[0:SQ, 0:2 * 2 * FF].bitcast(F32)
        hT = stage[:].rearrange("p a f -> p (a f)")[:, 0:2 * FT * SQ].bitcast(F16)
        rb = [xa[:], xr[:]]
        ob = [yo[:], x2[:]]

        bank = stack.enter_context(nc.psum_tensor("bank", [128, 8, 512], F32))
        flat = bank[:].rearrange("p a f -> p (a f)")
        PTB = 4 * 512
        ob_ = bank[:, 6, :]
        misc = bank[:, 7, :]

        names = ("w_loaded const_loaded g_loaded setup_pool setup_dve setup_act x_loaded ctx_loaded mask_loaded xr_loaded "
                 "k_written q_written k_stacked q_stacked res_written x2_written "
                 "chunk_loaded0 chunk_loaded1 scaled hi_done lo_done "
                 "pe_s dve_max act_exp pe_t act_pt pe_pv dve_o misc_full misc_free "
                 "khi_done klo_done qf_done qhi_done qlo_done kv_ready mask_ready ln1_var ln1_rstd xn_done xa_used ctx_used mask_used "
                 "vpad_ready rexp_done ot_done ln2_var ln2_rstd x2_done x2hi_done x2lo_done res_done xr_used pool_chain "
                 "h_full h_act lg_full e_done idx_done idx_loaded route_done wcur_done w_full "
                 "dve_passed pool_passed dve_step g1_done gelu_done ht_full hthi_done htlo_done g2_done y_done r_loaded x2b_loaded out_written").split()
        s = {n: sem(n) for n in names}
        chunk_loaded = [s["chunk_loaded0"], s["chunk_loaded1"]]

        def view_w(ap):
            return ap.rearrange("(t p) n -> p t n", p=128)

        block = stack.enter_context(nc.Block())

        def chunk_dst(z, c, hl):
            t = wa if c < 2 else wb
            return t[:, bass.ds(z * (4 * CHUNK) + hl * (2 * CHUNK) + (c % 2) * CHUNK, CHUNK)]

        def alone(eng, sem_, n, passed):
            eng.wait_ge(sem_, n)
            eng.sem_inc(passed, 1)

        def over_batches(eng, body):
            body(0, 0)
            with eng.Fori(0, (B - 2) // 2) as i:
                body(i * 2 + 1, 1)
                body(i * 2 + 2, 0)
            body(B - 1, 1)

        @block.sync
        def _(sp):
            for n in ("xr_used", "x2_written", "res_written", "y_done"):
                sp.sem_inc(s[n], 1)
            for n, w in enumerate((Wq, Wk, Wv, Wo)):
                sp.dma_start(wqkvo[:, n, :, :], view_w(w)).then_inc(s["w_loaded"], 16)

            def load_prep(b):
                sp.dma_start(ctx_s[:, :, :], ctx[bass.ds(b, 1), :, :].rearrange("o (c r) d -> r (o c) d", r=CK)).then_inc(s["ctx_loaded"], 16)
                sp.dma_start(xa[:, :], x[bass.ds(b, 1), :, :].rearrange("o s d -> (o s) d")).then_inc(s["x_loaded"], 16)
                sp.dma_start(mask_s[:, :], mask[bass.ds(b, 1), :, :].rearrange("o s d -> (o s) d")).then_inc(s["mask_loaded"], 16)

            def load_chunk(b, c):
                if not (isinstance(b, int) and b == 0 and c < 2):
                    sp.wait_ge(s["lo_done"], b * CHUNKS + c - 1)
                if c < 2:
                    src = Wa[bass.ds(b, 1), c * 128:(c + 1) * 128, :].rearrange("o p f -> (o p) f")
                    dst = stage[:, c % 2, :]
                else:
                    src = Wb[bass.ds(b, 1), (c - 2) * 512:(c - 1) * 512, :].rearrange("o (f p) n -> p (o f) n", p=128)
                    dst = stage[:, c % 2, :].rearrange("p (f n) -> p f n", n=D)
                sp.dma_start(dst, src).then_inc(chunk_loaded[c % 2], 16)

            def stack_q(b, par):
                sp.wait_ge(s["qlo_done"], b + 1)
                for a in range(2):
                    sp.dma_start(q_scr[bass.ds(b, 1), a, :, :, :].rearrange("o r (t j) f -> j r (o t) f", t=DT),
                                 q_hl[:, a, :].rearrange("p (t f) -> p t f", t=DT)).then_inc(s["q_written"], 16)

            def stack_k(b, t):
                sp.wait_ge(s["klo_done"], b * 2 + t + 1)
                sp.dma_start(k_scr[bass.ds(b, 1), :, :, 4 * t:4 * t + 4, :].rearrange("o r a j f -> j (o r) a f"),
                             k_hl[:, t, :, :]).then_inc(s["k_written"], 16)

            def read_stacks(b, par):
                sp.wait_ge(s["k_written"], b * 32 + 32)
                for p in range(2):
                    for a in range(2):
                        src = bass.AP(k_scr.tensor, b * (64 * PAIRS * SK) + (p * 32 + a) * (PAIRS * SK),
                                      [[0, 2], [2 * PAIRS * SK, 16], [1, PAIRS * SK]])
                        sp.dma_start(kst[64 * p + 32 * a:64 * p + 32 * a + 32, par, :], src).then_inc(s["k_stacked"], 16)
                sp.wait_ge(s["q_written"], b * 32 + 32)
                for p in range(2):
                    for a in range(2):
                        src = bass.AP(q_scr.tensor, b * (2 * 32 * PAIRS * SQ) + p * (16 * PAIRS * SQ),
                                      [[32 * PAIRS * SQ, 2], [PAIRS * SQ, 16], [1, PAIRS * SQ]])
                        sp.dma_start(qst[64 * p + 32 * a:64 * p + 32 * a + 32, par, :, :].rearrange("p a f -> p (a f)"),
                                     src).then_inc(s["q_stacked"], 16)

            load_prep(0)
            stack_k(0, 0)
            stack_k(0, 1)
            stack_q(0, 0)
            read_stacks(0, 0)
            sp.wait_ge(s["xn_done"], 1)
            sp.wait_ge(s["xa_used"], 1)
            sp.wait_ge(s["ctx_used"], 1)
            sp.wait_ge(s["mask_ready"], 1)
            load_prep(1)

            def body(b, par):
                first = isinstance(b, int) and b == 0
                last = isinstance(b, int) and b == B - 1
                load_chunk(b, 0)
                load_chunk(b, 1)
                if not first:
                    sp.wait_ge(s["xr_used"], b)
                    sp.dma_start(xr[:, :], x[bass.ds(b - 1, 1), :, :].rearrange("o s d -> (o s) d")).then_inc(s["xr_loaded"], 16)
                if not last:
                    stack_k(b + 1, 0)
                    stack_k(b + 1, 1)
                    stack_q(b + 1, 1 - par)
                    read_stacks(b + 1, 1 - par)
                load_chunk(b, 2)
                load_chunk(b, 3)
                if not last:
                    sp.wait_ge(s["xa_used"], b + 2)
                    sp.wait_ge(s["ctx_used"], b + 2)
                    sp.wait_ge(s["mask_ready"], b + 2)
                    if isinstance(b, int):
                        if b + 2 < B:
                            load_prep(b + 2)
                    else:
                        load_prep(b + 2)
                if not first:
                    store_post(b - 1)

            def store_post(b):
                sp.wait_ge(s["res_done"], b + 1)
                sp.dma_start(r_scr[bass.ds(b, 1), :, :].rearrange("o s d -> (o s) d"), res[:, :]).then_inc(s["res_written"], 16)
                sp.wait_ge(s["x2lo_done"], b + 1)
                sp.dma_start(x2_scr[bass.ds(b, 1), :, :].rearrange("o p f -> (o p) f"),
                             x2T[:].rearrange("p a f -> p (a f)")).then_inc(s["x2_written"], 16)

            body(0, 0)
            with sp.Fori(0, (B - 4) // 2) as i:
                body(i * 2 + 1, 1)
                body(i * 2 + 2, 0)
            for b in range(B - 3, B):
                body(b, b % 2)
            sp.wait_ge(s["xr_used"], B)
            sp.dma_start(xr[:, :], x[B - 1, :, :]).then_inc(s["xr_loaded"], 16)
            store_post(B - 1)

            sp.wait_ge(s["idx_done"], 1)
            sp.dma_start(idx_row[:, :], pidx[:, :]).then_inc(s["idx_loaded"], 16)
            sp.wait_ge(s["res_written"], 16 * B + 1)
            sp.wait_ge(s["x2_written"], 16 * B + 1)

            def load_ffn(b, par):
                sp.dma_start(rb[par], r_scr[bass.ds(b, 1), :, :].rearrange("o s d -> (o s) d")).then_inc(s["r_loaded"], 16)
                sp.dma_start(x2b[:, par, :], x2_scr[bass.ds(b, 1), :, :].rearrange("o p f -> (o p) f")).then_inc(s["x2b_loaded"], 16)

            def store_out(b, par):
                sp.wait_ge(s["y_done"], b + 2)
                sp.dma_start(out[bass.ds(b, 1), :, :].rearrange("o s d -> (o s) d"), ob[par]).then_inc(s["out_written"], 16)

            load_ffn(0, 0)
            sp.wait_ge(s["r_loaded"], 16)
            sp.wait_ge(s["x2b_loaded"], 16)
            load_ffn(1, 1)
            with sp.Fori(0, (B - 2) // 2) as i:
                for par in range(2):
                    b = i * 2 + par
                    store_out(b, par)
                    sp.wait_ge(s["r_loaded"], b * 16 + 32)
                    sp.wait_ge(s["x2b_loaded"], b * 16 + 32)
                    load_ffn(b + 2, par)
            store_out(B - 2, 0)
            store_out(B - 1, 1)
            sp.wait_ge(s["out_written"], 16 * B)

        @block.gpsimd
        def _(pool):
            g = nc.gpsimd
            chain = Steps(pool, s["pool_chain"])
            g.dma_start(bq_c[:, :], bq.rearrange("(t p) -> p t", p=128), allow_slow_non_contiguous=True).then_inc(s["const_loaded"], 16)
            g.dma_start(bk_c[:, :], bk.rearrange("(t p) -> p t", p=128), allow_slow_non_contiguous=True).then_inc(s["const_loaded"], 16)
            g.dma_start(bv_r[:, :], bass.AP(bv.tensor, 0, [[0, 128], [1, D]])).then_inc(s["const_loaded"], 16)
            g.dma_start(bo_r[:, :], bass.AP(bo.tensor, 0, [[0, 128], [1, D]])).then_inc(s["const_loaded"], 16)
            g.dma_start(w1_s[:, :, :], W1.rearrange("(t p) n -> p t n", p=128)).then_inc(s["const_loaded"], 16)
            g.dma_start(w2_s[:, :], W2).then_inc(s["const_loaded"], 16)
            g.dma_start(b1_c[:, :], b1.rearrange("(p o) -> p o", o=1), allow_slow_non_contiguous=True).then_inc(s["const_loaded"], 16)
            g.dma_start(b2_r[:, :], bass.AP(b2.tensor, 0, [[0, B], [1, NZ]])).then_inc(s["const_loaded"], 16)
            g.dma_start(gates[:, 0:1], bass.AP(g_xattn.tensor, 0, [[0, 128], [1, 1]])).then_inc(s["g_loaded"], 16)
            g.dma_start(gates[:, 1:2], bass.AP(g_ffn.tensor, 0, [[0, 128], [1, 1]])).then_inc(s["g_loaded"], 16)
            chain.link(g.memset(ident[:, :], 0.0))
            chain.link(g.affine_select(out=ident[:, :], in_=ident[:, :], compare_op=ALU.not_equal, fill=1.0,
                                       base=0, pattern=[[-1, 128]], channel_multiplier=1))
            chain.link(g.tensor_copy(ident_b[:, :], ident[0:SQ, 0:SQ]))
            chain.link(g.memset(half[:, :], -0.5))
            chain.link(g.memset(ones[:, :], 1.0))
            g.memset(vpad[:].rearrange("p a b c -> p (a b c)"), 0.0).then_inc(s["setup_pool"], 1)

            def pow_rstd(dst, src, ready, n, signal):
                pool.wait_ge(ready, n)
                g.tensor_tensor(dst, src, half[0:SQ, :], ALU.pow).then_inc(signal, 1)

            def scale_chunk(b, c):
                st = stage[:, c % 2, :]
                alone(pool, chunk_loaded[c % 2], b * 32 + 16 * (c // 2) + 16, s["pool_passed"])
                g.tensor_scalar(st, st, WSCALE, 1.0, ALU.mult, ALU.mult).then_inc(s["scaled"], 1)

            def lo_chunk(b, c):
                alone(pool, s["hi_done"], b * CHUNKS + c + 1, s["pool_passed"])
                g.tensor_tensor(chunk_dst(b, c, 1), stage[:, c % 2, :], chunk_dst(b, c, 0), ALU.subtract).then_inc(s["lo_done"], 1)

            pow_rstd(rstd[:, :], ve[:, :], s["ln1_var"], 1, s["ln1_rstd"])

            def body(b, par):
                first = isinstance(b, int) and b == 0
                last = isinstance(b, int) and b == B - 1
                if not last:
                    pow_rstd(rstd[:, :], ve[:, :], s["ln1_var"], b + 2, s["ln1_rstd"])
                scale_chunk(b, 0)
                lo_chunk(b, 0)
                scale_chunk(b, 1)
                lo_chunk(b, 1)
                scale_chunk(b, 2)
                if not first:
                    pow_rstd(rstd2[:, :], ve2[:, :], s["ln2_var"], b, s["ln2_rstd"])
                lo_chunk(b, 2)
                scale_chunk(b, 3)
                lo_chunk(b, 3)

            over_batches(pool, body)
            pow_rstd(rstd2[:, :], ve2[:, :], s["ln2_var"], B, s["ln2_rstd"])

        @block.scalar
        def _(act):
            a = nc.scalar
            act.wait_ge(s["g_loaded"], 32)
            a.activation(tgate[:, :], gates[:, :], ACT.Tanh).then_inc(s["setup_act"], 1)

            def exp_pair(b, par, p):
                act.wait_ge(s["dve_max"], b * PAIRS + p + 1)
                if not (isinstance(b, int) and b == 0 and p < 2):
                    act.wait_ge(s["pe_t"], b * PAIRS + p - 1)
                for e in range(2):
                    h = 2 * p + e
                    ins = a.activation(probs[:, p % 2, e, :], bank[0:SQ, 2 * (p % 2) + e, 0:SK], ACT.Exp,
                                       bias=negmax[:, h:h + 1], accum_out=rowsum[:, par, h:h + 1])
                ins.then_inc(s["act_exp"], 1)

            def pt_copy(b, p):
                act.wait_ge(s["pe_t"], b * PAIRS + p + 1)
                if not (isinstance(b, int) and b == 0 and p < 2):
                    act.wait_ge(s["pe_pv"], b * PAIRS + p - 1)
                a.activation(pT[:, p % 2, :, :], flat[0:CK, PTB:PTB + KC * 256].rearrange("p (c f) -> p c f", c=KC)[:, :, 0:2 * SQ],
                             ACT.Copy).then_inc(s["act_pt"], 1)

            def k_hi(b, t, use):
                act.wait_ge(s["misc_full"], use)
                if not (isinstance(b, int) and b == 0):
                    act.wait_ge(s["k_written"], b * 32)
                a.activation(k_hl[:, t, 0, :], misc[:, 0:SK], ACT.Identity, bias=bk_c[:, t:t + 1]).then_inc(s["khi_done"], 1)

            def q_hi(b):
                act.wait_ge(s["qf_done"], b + 1)
                if not (isinstance(b, int) and b == 0):
                    act.wait_ge(s["q_written"], b * 32)
                a.activation(q_hl[:, 0, :], q_f[:, :], ACT.Copy).then_inc(s["qhi_done"], 1)

            def x2_hi(b, use):
                act.wait_ge(s["misc_full"], use)
                if not (isinstance(b, int) and b == 0):
                    act.wait_ge(s["x2_written"], b * 16 + 1)
                a.activation(x2T[:, 0, :], misc[:, 0:DT * SQ], ACT.Copy).then_inc(s["x2hi_done"], 1)

            act.wait_ge(s["const_loaded"], 128)
            k_hi(0, 0, 3)
            k_hi(0, 1, 4)
            q_hi(0)
            exp_pair(0, 0, 0)
            exp_pair(0, 0, 1)

            def body(b, par):
                first = isinstance(b, int) and b == 0
                last = isinstance(b, int) and b == B - 1
                u = uses_before(b) + (0 if first else 1) + V_USES
                for p in range(PAIRS):
                    pt_copy(b, p)
                    if p < PAIRS - 2:
                        exp_pair(b, par, p + 2)
                    if p == 2 and not last:
                        k_hi(b + 1, 0, u + 3)
                        k_hi(b + 1, 1, u + 4)
                    if p == 3 and not last:
                        q_hi(b + 1)
                    if p == 5 and not first:
                        x2_hi(b - 1, u + (0 if last else PREP_USES) + 2)
                    if p >= PAIRS - 2 and not last:
                        exp_pair(b + 1, 1 - par, p - PAIRS + 2)

            over_batches(act, body)
            x2_hi(B - 1, uses_before(B - 1) + POST_USES + V_USES + 3)
            act.wait_ge(s["h_full"], 1)
            a.activation(h_s[:, :], misc[0:RH, 0:B], ACT.Tanh, bias=b1_c[:, :], scale=1.0 / SQ).then_inc(s["h_act"], 1)
            act.wait_ge(s["lg_full"], 2)
            a.activation(ez[:, :], lg[:, :], ACT.Exp, bias=nmx[:, :], accum_out=zs[:, :]).then_inc(s["e_done"], 1)
            act.wait_ge(s["route_done"], 1)

            def gelu(u_done, hf):
                act.wait_ge(s["g1_done"], u_done * 2 + hf + 1)
                act.wait_ge(s["ht_full"], u_done * 2)
                a.activation(h_f[:, hf * 512:(hf + 1) * 512], bank[0:SQ, hf, :], ACT.Gelu_apprx_tanh,
                             scale=1.0 / WSCALE).then_inc(s["gelu_done"], 1)

            def ht_hi(b, par, k, hf):
                u = b * TOPK + k
                if k == 0 and hf == 0:
                    act.wait_ge(s["wcur_done"], b + 1)
                act.wait_ge(s["ht_full"], u * 2 + hf + 1)
                if not (isinstance(u, int) and u == 0):
                    act.wait_ge(s["g2_done"], u)
                a.activation(hT[:, hf * 448:hf * 448 + 448], bank[:, 2 + hf, 0:448], ACT.Copy,
                             scale=wcur[:, par, k:k + 1]).then_inc(s["hthi_done"], 1)

            def ffn_body(b, par, last):
                for k in range(TOPK):
                    u = b * TOPK + k
                    for hf in range(2):
                        ht_hi(b, par, k, hf)
                        if not (last and k == TOPK - 1):
                            gelu(u + 1, hf)

            gelu(0, 0)
            gelu(0, 1)
            ffn_body(0, 0, False)
            with act.Fori(0, (B - 2) // 2) as i:
                ffn_body(i * 2 + 1, 1, False)
                ffn_body(i * 2 + 2, 0, False)
            ffn_body(B - 1, 1, True)

        N_MAX, N_V, N_PREP, N_POST = PAIRS, 3, 0, 0

        @block.vector
        def _(dve):
            v = nc.vector
            st = Steps(dve, s["dve_step"])
            tot = [0]
            dve.wait_ge(s["w_loaded"], 64)
            dve.wait_ge(s["const_loaded"], 128)
            dve.wait_ge(s["setup_act"], 1)
            st.link(v.tensor_scalar(wqkvo[:, 0, :, :], wqkvo[:, 0, :, :], HD ** -0.5, None, ALU.mult))
            st.link(v.tensor_scalar(bq_c[:, :], bq_c[:, :], HD ** -0.5, None, ALU.mult))
            st.link(v.tensor_scalar(tf_w[:, :], tgate[:, 1:2], 1.0 / WSCALE, None, ALU.mult))
            v.memset(x2T[:].rearrange("p a f -> p (a f)"), 0.0).then_inc(s["setup_dve"], 1)
            dve.wait_ge(s["setup_dve"], 1)

            def mask_bias(b, par):
                dve.wait_ge(s["mask_loaded"], b * 16 + 16)
                if not (isinstance(b, int) and b < 2):
                    dve.wait_ge(s["pe_s"], b * PAIRS - PAIRS)
                v.tensor_scalar(maskb[:, par, :], mask_s[:, :], MASKED, 1.0, ALU.mult, ALU.mult).then_inc(s["mask_ready"], 1)

            def row_max(b, p):
                dve.wait_ge(s["pe_s"], b * PAIRS + p + 1)
                v.tensor_reduce(negmax[:, 2 * p:2 * p + 2], bank[0:SQ, 2 * (p % 2):2 * (p % 2) + 2, 0:SK], AX.X, ALU.max,
                                negate=True).then_inc(s["dve_max"], 1)

            def use(n):
                dve.wait_ge(s["misc_full"], n)

            def layernorm_stats(src, stat_, mv_, ve_, ready):
                st.link(v.bn_stats(stat_[:, :], src))
                dve.sem_inc(s["dve_passed"], 1)
                st.link(v.bn_aggr(mv_[:, :], stat_[:, :]))
                v.tensor_scalar(ve_[:, :], mv_[:, 1:2], EPS, None, ALU.add).then_inc(ready, 1)

            def ln1_stats(b):
                dve.wait_ge(s["x_loaded"], b * 16 + 16)
                layernorm_stats(xa[:, :], stat, mv, ve, s["ln1_var"])

            def ln1_apply(b):
                dve.wait_ge(s["ln1_rstd"], b + 1)
                v.tensor_scalar(xa[:, :], xa[:, :], mv[:, 0:1], rstd[:, :], ALU.subtract, ALU.mult).then_inc(s["xn_done"], 1)

            def ctx_copy(n, t):
                use(n)
                v.tensor_copy(ctxT[:, t, :], misc[:, 0:SK]).then_inc(s["misc_free"], 1)

            def x_copy(b, n):
                use(n)
                v.tensor_copy(xT[:, :], misc[:, 0:DT * SQ]).then_inc(s["misc_free"], 1)

            def k_lo(b, t, n):
                dve.wait_ge(s["khi_done"], b * 2 + t + 1)
                ins = v.scalar_tensor_tensor(out=k_hl[:, t, 1, :], in0=misc[:, 0:SK], scalar=bk_c[:, t:t + 1],
                                             in1=k_hl[:, t, 0, :], op0=ALU.add, op1=ALU.subtract)
                ins.then_inc(s["klo_done"], 1)
                dve.wait_ge(s["klo_done"], b * 2 + t + 1)
                dve.sem_inc(s["misc_free"], 1)

            def q_full(b, n):
                use(n)
                if not (isinstance(b, int) and b == 0):
                    dve.wait_ge(s["q_written"], b * 32)
                for t in range(DT):
                    ins = v.tensor_scalar(q_f[:, t * SQ:(t + 1) * SQ], misc[:, t * SQ:(t + 1) * SQ], bq_c[:, t:t + 1], None, ALU.add)
                    if t == 0:
                        st.done(ins)
                ins.then_inc(s["qf_done"], 1)
                dve.wait_ge(s["qf_done"], b + 1)
                dve.sem_inc(s["misc_free"], 1)

            def q_lo(b):
                dve.wait_ge(s["qhi_done"], b + 1)
                v.tensor_tensor(q_hl[:, 1, :], q_f[:, :], q_hl[:, 0, :], ALU.subtract).then_inc(s["qlo_done"], 1)

            def v_copy(c, off, signal):
                out_ = bass.AP(vpad, c * PAIRS * 64, [[KC * PAIRS * 64, CK], [64, PAIRS], [48, 2], [1, HD]])
                return v.tensor_tensor(out_, misc[0:CK, off:off + D].rearrange("p (q e i) -> p q e i", e=2, i=HD),
                                       bv_r[0:CK, :].rearrange("p (q e i) -> p q e i", e=2, i=HD), ALU.add)

            def v_stage(b, n):
                if not (isinstance(b, int) and b == 0):
                    dve.wait_ge(s["pe_pv"], b * PAIRS)
                use(n)
                st.done(v_copy(0, 0, None))
                v_copy(1, D, None).then_inc(s["misc_free"], 1)
                use(n + 1)
                st.done(v_copy(2, 0, None))
                dve.wait_ge(s["dve_step"], st.base + st.n)
                dve.wait_ge(s["misc_free"], n)
                dve.sem_inc(s["misc_free"], 1)
                dve.sem_inc(s["vpad_ready"], 1)

            def row_sums(b, par):
                dve.wait_ge(s["act_exp"], b * PAIRS + PAIRS)
                st.link(v.reciprocal(rinv[:, :], rowsum[:, par, :]))
                v.tensor_copy(rexp[:, :, :], bass.AP(rinv, 0, [[NH, SQ], [1, NH], [0, HD]])).then_inc(s["rexp_done"], 1)

            def rt_copy(n):
                use(n)
                v.tensor_copy(rT[:, :], misc[:, 0:DT * SQ]).then_inc(s["misc_free"], 1)
                dve.wait_ge(s["misc_free"], n)

            def o_scale(b):
                dve.wait_ge(s["pe_pv"], b * PAIRS + PAIRS)
                v.tensor_tensor(oT[:, :], ob_[:, 0:DT * SQ], rT[:, :], ALU.mult).then_inc(s["dve_o"], 1)

            def residual(b, n):
                use(n)
                v.tensor_tensor(yo[:, :], misc[0:SQ, 0:D], bo_r[0:SQ, :], ALU.add).then_inc(s["misc_free"], 1)
                dve.wait_ge(s["misc_free"], n)
                dve.wait_ge(s["xr_loaded"], b * 16 + 16)
                st.link(v.scalar_tensor_tensor(out=xr[:, :], in0=yo[:, :], scalar=tgate[0:SQ, 0:1], in1=xr[:, :], op0=ALU.mult, op1=ALU.add))
                layernorm_stats(xr[:, :], stat2, mv2, ve2, s["ln2_var"])

            def ln2_apply(b):
                dve.wait_ge(s["ln2_rstd"], b + 1)
                v.tensor_scalar(x2[:, :], xr[:, :], mv2[:, 0:1], rstd2[:, :], ALU.subtract, ALU.mult).then_inc(s["x2_done"], 1)
                dve.wait_ge(s["x2_done"], b + 1)
                if not (isinstance(b, int) and b == 0):
                    dve.wait_ge(s["res_written"], b * 16 + 1)
                v.scalar_tensor_tensor(out=res[:, :], in0=x2[:, :], scalar=tgate[0:SQ, 1:2], in1=xr[:, :], op0=ALU.mult,
                                       op1=ALU.add).then_inc(s["res_done"], 1)
                dve.wait_ge(s["res_done"], b + 1)
                dve.sem_inc(s["xr_used"], 1)

            def x2_lo(b, n):
                dve.wait_ge(s["x2hi_done"], b + 1)
                v.tensor_tensor(x2T[:, 1, :], misc[:, 0:DT * SQ], x2T[:, 0, :], ALU.subtract).then_inc(s["x2lo_done"], 1)
                dve.wait_ge(s["x2lo_done"], b + 1)
                v.tensor_reduce(pooled[:, :, bass.ds(b, 1)], misc[:, 0:DT * SQ].rearrange("p (t f) -> p t f", t=DT), AX.X,
                                ALU.add).then_inc(s["misc_free"], 1)

            def w_hi(b, c):
                alone(dve, s["scaled"], b * CHUNKS + c + 1, s["dve_passed"])
                v.tensor_copy(chunk_dst(b, c, 0), stage[:, c % 2, :]).then_inc(s["hi_done"], 1)

            mask_bias(0, 0)
            ctx_copy(1, 0)
            ctx_copy(2, 1)
            ln1_stats(0)
            k_lo(0, 0, 3)
            k_lo(0, 1, 4)
            ln1_apply(0)
            x_copy(0, 5)
            q_full(0, 6)
            q_lo(0)
            row_max(0, 0)
            row_max(0, 1)
            SET = st.n
            counts = {}

            def body(b, par):
                first = isinstance(b, int) and b == 0
                last = isinstance(b, int) and b == B - 1
                st.begin(SET if first else SET + FIRST + FULL * (b - 1))
                u = uses_before(b)
                for p in range(PAIRS):
                    if p < PAIRS - 2:
                        row_max(b, p + 2)
                    elif not last:
                        row_max(b + 1, p - PAIRS + 2)
                    if p == 0:
                        if not first:
                            rt_copy(u + 1)
                            o_scale(b - 1)
                            u = u + 1
                        v_stage(b, u + 1)
                        u = u + V_USES
                        if not last:
                            ln1_stats(b + 1)
                    if p == 1 and not last:
                        ctx_copy(u + 1, 0)
                        ctx_copy(u + 2, 1)
                        ln1_apply(b + 1)
                    if p == 2 and not last:
                        k_lo(b + 1, 0, u + 3)
                        k_lo(b + 1, 1, u + 4)
                    if p == 3:
                        if not last:
                            x_copy(b + 1, u + 5)
                            q_full(b + 1, u + 6)
                            u = u + PREP_USES
                            q_lo(b + 1)
                    if p == 3 and not last:
                        mask_bias(b + 1, 1 - par)
                    if p % 2 == 1:
                        w_hi(b, p // 2)
                    if p == 4:
                        if not first:
                            residual(b - 1, u + 1)
                    if p == 5:
                        if not first:
                            ln2_apply(b - 1)
                    if p == 6 and not first:
                        x2_lo(b - 1, u + 2)
                    if p == 7:
                        row_sums(b, par)
                counts["last" if last else "first" if first else "full"] = st.n

            FIRST, FULL = 6, 9
            over_batches(dve, body)
            assert counts["first"] == FIRST and counts["full"] == FULL, counts
            st.begin(SET + FIRST + FULL * (B - 2) + counts["last"])
            u = uses_before(B - 1) + 1 + V_USES + 2
            rt_copy(u + 1)
            o_scale(B - 1)
            residual(B - 1, u + 2)
            ln2_apply(B - 1)
            x2_lo(B - 1, u + 3)

            dve.wait_ge(s["lg_full"], 1)
            st.link(v.tensor_tensor(lg[:, :], misc[0:B, 0:NZ], b2_r[:, :], ALU.add))
            st.link(v.max(top[:, :], lg[:, :]))
            v.tensor_scalar(nmx[:, :], top[:, 0:1], -1.0, None, ALU.mult).then_inc(s["lg_full"], 1)
            dve.wait_ge(s["e_done"], 1)
            st.link(v.reciprocal(zr[:, :], zs[:, :]))
            st.link(v.tensor_scalar(pz[:, :], ez[:, :], zr[:, :], None, ALU.mult))
            st.link(v.max(ptop[:, :], pz[:, :]))
            v.max_index(pidx[:, :], ptop[:, :], pz[:, :]).then_inc(s["idx_done"], 1)
            st.link(v.tensor_reduce(ts[:, :], ptop[:, 0:TOPK], AX.X, ALU.add))
            st.link(v.reciprocal(tr[:, :], ts[:, :]))
            st.link(v.tensor_scalar(wz[:, :], ptop[:, 0:TOPK], tr[:, :], None, ALU.mult))
            v.tensor_tensor(wdiag[:, :, :], bass.AP(wz, 0, [[TOPK, B], [0, B], [1, TOPK]]),
                            bass.AP(ident, 0, [[128, B], [1, B], [0, TOPK]]), ALU.mult).then_inc(s["w_full"], 1)
            dve.wait_ge(s["w_full"], 2)
            v.tensor_copy(wbc[:, :], misc[:, 0:B * TOPK]).then_inc(s["route_done"], 1)
            dve.wait_ge(s["route_done"], 1)

            def ffn_body(b, par):
                v.tensor_copy(wcur[:, par, :], wbc[:, bass.ds(b * TOPK, TOPK)]).then_inc(s["wcur_done"], 1)
                dve.wait_ge(s["wcur_done"], b + 1)
                for k in range(TOPK):
                    u = b * TOPK + k
                    for hf in range(2):
                        dve.wait_ge(s["hthi_done"], u * 2 + hf + 1)
                        v.scalar_tensor_tensor(out=hT[:, FT * SQ + hf * 448:FT * SQ + hf * 448 + 448], in0=bank[:, 2 + hf, 0:448],
                                               scalar=wcur[:, par, k:k + 1], in1=hT[:, hf * 448:hf * 448 + 448],
                                               op0=ALU.mult, op1=ALU.subtract).then_inc(s["htlo_done"], 1)
                dve.wait_ge(s["g2_done"], b * TOPK + TOPK)
                dve.wait_ge(s["r_loaded"], b * 16 + 16)
                if not isinstance(b, int):
                    dve.wait_ge(s["out_written"], b * 16 - 16)
                v.scalar_tensor_tensor(out=ob[par], in0=bank[0:SQ, 4 + par, 0:D], scalar=tf_w[0:SQ, :], in1=rb[par],
                                       op0=ALU.mult, op1=ALU.add).then_inc(s["y_done"], 1)

            ffn_body(0, 0)
            ffn_body(1, 1)
            with dve.Fori(0, (B - 2) // 2) as i:
                for par in range(2):
                    b = i * 2 + 2 + par
                    ffn_body(b, par)

        @block.tensor
        def _(pe):
            T = nc.tensor
            wq_s, wk_s, wv_s, wo_s = (wqkvo[:, n, :, :] for n in range(4))
            pe.wait_ge(s["setup_pool"], 1)
            pe.wait_ge(s["setup_dve"], 1)

            def use(n):
                if not (isinstance(n, int) and n == 1):
                    pe.wait_ge(s["misc_free"], n - 1)

            def full(ins):
                ins.then_inc(s["misc_full"], 1)

            def scores(b, par, p):
                if p == 0:
                    pe.wait_ge(s["k_stacked"], b * 64 + 64)
                    pe.wait_ge(s["q_stacked"], b * 64 + 64)
                    pe.wait_ge(s["mask_ready"], b + 1)
                if not (isinstance(b, int) and b == 0 and p < 2):
                    pe.wait_ge(s["act_exp"], b * PAIRS + p - 1)
                for e in range(2):
                    o = bank[0:SQ, 2 * (p % 2) + e, 0:SK]
                    T.matmul(o, ident_b[:, :], maskb[:, par, :], start=True, stop=False)
                for e in range(2):
                    o = bank[0:SQ, 2 * (p % 2) + e, 0:SK]
                    ins = T.matmul(o, qst[64 * e:64 * e + 64, par, p, :], kst[64 * e:64 * e + 64, par, p * SK:(p + 1) * SK],
                                   start=False, stop=True)
                ins.then_inc(s["pe_s"], 1)

            def transpose_probs(b, p):
                pe.wait_ge(s["act_exp"], b * PAIRS + p + 1)
                if not (isinstance(b, int) and b == 0 and p == 0):
                    pe.wait_ge(s["act_pt"], b * PAIRS + p)
                for e in range(2):
                    for c in range(KC):
                        o = PTB + c * 256 + e * SQ
                        ins = T.transpose(flat[0:CK, o:o + SQ], probs[:, p % 2, e, c * CK:(c + 1) * CK], ident[0:SQ, 0:SQ])
                ins.then_inc(s["pe_t"], 1)

            def pv(b, p):
                t, j = p // 4, p % 4
                pe.wait_ge(s["act_pt"], b * PAIRS + p + 1)
                if p == 0:
                    pe.wait_ge(s["vpad_ready"], b + 1)
                    if not (isinstance(b, int) and b == 0):
                        pe.wait_ge(s["dve_o"], b)
                o = bank[32 * j:32 * j + 32, 6, t * SQ:(t + 1) * SQ]
                for e in range(2):
                    for c in range(KC):
                        ins = T.matmul(o, vpad[:, c, p, 32 * e:32 * e + 32], pT[:, p % 2, c, e * SQ:(e + 1) * SQ],
                                       start=(e == 0 and c == 0), stop=(e == 1 and c == KC - 1))
                ins.then_inc(s["pe_pv"], 1)

            def ctx_t(b, t, n):
                use(n)
                if t == 0:
                    pe.wait_ge(s["ctx_loaded"], b * 16 + 16)
                for c in range(KC):
                    ins = T.transpose(misc[:, c * CK:(c + 1) * CK], ctx_s[:, c, t * 128:(t + 1) * 128], ident[0:CK, 0:CK])
                full(ins)
                if t == 1:
                    ctx_mark(b, n)

            def ctx_mark(b, n):
                pe.wait_ge(s["misc_full"], n)
                pe.sem_inc(s["ctx_used"], 1)

            def k_proj(t, n):
                use(n)
                for kt in range(DT):
                    ins = T.matmul(misc[:, 0:SK], wk_s[:, kt, t * 128:(t + 1) * 128], ctxT[:, kt, :], start=(kt == 0), stop=(kt == DT - 1))
                full(ins)

            def x_t(b, n):
                pe.wait_ge(s["xn_done"], b + 1)
                use(n)
                for t in range(DT):
                    ins = T.transpose(misc[:, t * SQ:(t + 1) * SQ], xa[:, t * 128:(t + 1) * 128], ident[0:SQ, 0:SQ])
                full(ins)
                pe.wait_ge(s["misc_full"], n)
                pe.sem_inc(s["xa_used"], 1)

            def q_proj(n):
                use(n)
                for t in range(DT):
                    for kt in range(DT):
                        ins = T.matmul(misc[:, t * SQ:(t + 1) * SQ], wq_s[:, kt, t * 128:(t + 1) * 128], xT[:, kt * SQ:(kt + 1) * SQ],
                                       start=(kt == 0), stop=(kt == DT - 1))
                full(ins)

            def v_proj(n):
                for cs in ((0, 1), (2,)):
                    use(n)
                    for c in cs:
                        for kt in range(DT):
                            ins = T.matmul(misc[0:CK, (c % 2) * D:(c % 2 + 1) * D], ctxT[:, kt, c * CK:(c + 1) * CK], wv_s[:, kt, :],
                                           start=(kt == 0), stop=(kt == DT - 1))
                    full(ins)
                    n = n + 1

            def r_t(b, n):
                pe.wait_ge(s["rexp_done"], b + 1)
                use(n)
                for t in range(DT):
                    ins = T.transpose(misc[:, t * SQ:(t + 1) * SQ], rexp[:].rearrange("p h i -> p (h i)")[:, t * 128:(t + 1) * 128],
                                      ident[0:SQ, 0:SQ])
                full(ins)

            def o_proj(b, n):
                pe.wait_ge(s["dve_o"], b + 1)
                use(n)
                for t in range(DT):
                    ins = T.matmul(misc[0:SQ, 0:D], oT[:, t * SQ:(t + 1) * SQ], wo_s[:, t, :], start=(t == 0), stop=(t == DT - 1))
                full(ins)

            def x2_t(b, n):
                pe.wait_ge(s["x2_done"], b + 1)
                use(n)
                for t in range(DT):
                    ins = T.transpose(misc[:, t * SQ:(t + 1) * SQ], x2[:, t * 128:(t + 1) * 128], ident[0:SQ, 0:SQ])
                full(ins)

            ctx_t(0, 0, 1)
            ctx_t(0, 1, 2)
            k_proj(0, 3)
            k_proj(1, 4)
            x_t(0, 5)
            q_proj(6)
            scores(0, 0, 0)
            scores(0, 0, 1)

            def body(b, par):
                first = isinstance(b, int) and b == 0
                last = isinstance(b, int) and b == B - 1
                u = uses_before(b)
                for p in range(PAIRS):
                    transpose_probs(b, p)
                    if p < PAIRS - 2:
                        scores(b, par, p + 2)
                    elif not last:
                        scores(b + 1, 1 - par, p - PAIRS + 2)
                    if p == 0:
                        if not first:
                            r_t(b - 1, u + 1)
                            pv(b - 1, PAIRS - 1)
                            u = u + 1
                        v_proj(u + 1)
                        u = u + V_USES
                    else:
                        pv(b, p - 1)
                    if not last:
                        if p == 1:
                            ctx_t(b + 1, 0, u + 1)
                            ctx_t(b + 1, 1, u + 2)
                        if p == 2:
                            k_proj(0, u + 3)
                            k_proj(1, u + 4)
                        if p == 3:
                            x_t(b + 1, u + 5)
                            q_proj(u + 6)
                            u = u + PREP_USES
                    if not first:
                        if p == 4:
                            o_proj(b - 1, u + 1)
                        if p == 6:
                            x2_t(b - 1, u + 2)

            over_batches(pe, body)
            u = uses_before(B - 1) + 1 + V_USES + 2
            r_t(B - 1, u + 1)
            pv(B - 1, PAIRS - 1)
            o_proj(B - 1, u + 2)
            x2_t(B - 1, u + 3)

            pe.wait_ge(s["misc_free"], u + 3)
            for t in range(DT):
                ins = T.matmul(misc[0:RH, 0:B], w1_s[:, t, :], pooled[:, t, :], start=(t == 0), stop=(t == DT - 1))
            ins.then_inc(s["h_full"], 1)
            pe.wait_ge(s["h_act"], 1)
            T.matmul(misc[0:B, 0:NZ], h_s[:, :], w2_s[:, :], start=True, stop=True).then_inc(s["lg_full"], 1)
            pe.wait_ge(s["w_full"], 1)
            T.matmul(misc[:, 0:B * TOPK], ones[:, :], wdiag[:].rearrange("p a b -> p (a b)"), start=True, stop=True).then_inc(s["w_full"], 1)
            pe.wait_ge(s["idx_loaded"], 16)
            pe.wait_ge(s["hi_done"], NCH)
            pe.wait_ge(s["lo_done"], NCH)

            def zone(b, k):
                return pe.value_load(idx_row[0:1, bass.ds(b * NZ + k, 1)], min_val=0, max_val=NZ - 1)

            def g1(b, par, k, e, hf):
                u = b * TOPK + k
                if k == 0 and hf == 0:
                    pe.wait_ge(s["x2b_loaded"], b * 16 + 16)
                if not (isinstance(u, int) and u == 0):
                    pe.wait_ge(s["gelu_done"], u * 2 - 1 + hf)
                o = bank[0:SQ, hf, :]
                n = 0
                for t in range(DT):
                    for xs, ws in ((0, 0), (0, 1), (1, 0)):
                        ins = T.matmul(o, x2b[:, par, xs * DT * SQ + t * SQ:xs * DT * SQ + (t + 1) * SQ],
                                       wa[:, bass.ds(e * (4 * CHUNK) + ws * (2 * CHUNK) + t * CHUNK + hf * 512, 512)],
                                       start=(n == 0), stop=(n == 3 * DT - 1))
                        n += 1
                ins.then_inc(s["g1_done"], 1)

            def ht(b, k, hf):
                u = b * TOPK + k
                pe.wait_ge(s["gelu_done"], u * 2 + hf + 1)
                if not (isinstance(u, int) and u == 0):
                    pe.wait_ge(s["htlo_done"], u * 2 - 1 + hf)
                for f in range(4):
                    ins = T.transpose(bank[:, 2 + hf, f * SQ:(f + 1) * SQ], h_f[:, hf * 512 + f * 128:hf * 512 + (f + 1) * 128],
                                      ident[0:SQ, 0:SQ])
                ins.then_inc(s["ht_full"], 1)

            def g2(b, par, k, e):
                u = b * TOPK + k
                if k == 0 and not (isinstance(b, int) and b < 2):
                    pe.wait_ge(s["y_done"], b)
                o = bank[0:SQ, 4 + par, 0:D]
                for f in range(FT):
                    if f % 4 == 0:
                        pe.wait_ge(s["htlo_done"], u * 2 + f // 4 + 1)
                    for hs, ws in ((0, 0), (0, 1), (1, 0)):
                        ins = T.matmul(o, hT[:, hs * FT * SQ + f * SQ:hs * FT * SQ + (f + 1) * SQ],
                                       wb[:, bass.ds(e * (4 * CHUNK) + ws * (2 * CHUNK) + f * D, D)],
                                       start=(k == 0 and f == 0 and hs == 0 and ws == 0), stop=(k == TOPK - 1 and f == FT - 1 and hs == 1))
                ins.then_inc(s["g2_done"], 1)

            def ffn_body(b, par, last):
                es = [zone(b, k) for k in range(TOPK)]
                for k in range(TOPK):
                    ht(b, k, 0)
                    if k < TOPK - 1:
                        nxt = (b, par, k + 1, es[k + 1])
                    elif not last:
                        nxt = (b + 1, 1 - par, 0, zone(b + 1, 0))
                    else:
                        nxt = None
                    if nxt:
                        g1(*nxt, 0)
                    ht(b, k, 1)
                    if nxt:
                        g1(*nxt, 1)
                    g2(b, par, k, es[k])

            e0 = zone(0, 0)
            g1(0, 0, 0, e0, 0)
            g1(0, 0, 0, e0, 1)
            ffn_body(0, 0, False)
            with pe.Fori(0, (B - 2) // 2) as i:
                ffn_body(i * 2 + 1, 1, False)
                ffn_body(i * 2 + 2, 0, False)
            ffn_body(B - 1, 1, True)


_INS = ["x", "ctx_1024", "mask_Bx1xSxS2_bk1", "g_xattn", "g_ffn", "L0_xattn_Wq", "L0_xattn_bq", "L0_xattn_Wk", "L0_xattn_bk",
        "L0_xattn_Wv", "L0_xattn_bv", "L0_xattn_Wo", "L0_xattn_bo", "L0_ffn_W1", "L0_ffn_b1", "L0_ffn_W2", "L0_ffn_b2",
        "L0_ffn_Wa", "L0_ffn_Wb"]


def kernel(**inputs):
    import numpy as np
    import concourse.bacc as bacc
    from concourse.bass_utils import run_bass_kernel_spmd as run

    nc = bacc.Bacc("TRN2", target_bir_lowering=False, num_devices=1)
    arrays, args = {}, []
    for name in _INS:
        a = np.ascontiguousarray(inputs[name])
        if a.dtype == np.bool_:
            a = a.reshape(B, SQ, SK)
        arrays[f"in_{name}"] = a
        args.append(nc.dram_tensor(f"in_{name}", a.shape, mybir.dt.from_np(a.dtype), kind="ExternalInput").ap())
    args.append(nc.dram_tensor("out_0", (B, SQ, D), F32, kind="ExternalOutput").ap())
    flamingo_layer(nc, *args)
    r = run(nc, [arrays], core_ids=[0])
    return r.results[0]["out_0"]
```

```python
from contextlib import ExitStack

import concourse.bass as bass
from concourse import mybir

F32 = mybir.dt.float32
F16 = mybir.dt.float16
BF16 = mybir.dt.bfloat16
U8 = mybir.dt.uint8
U32 = mybir.dt.uint32
ALU = mybir.AluOpType
ACT = mybir.ActivationFunctionType
AX = mybir.AxisListType

B, SQ, D, SK = 8, 112, 256, 375
NH, HD = 16, 16
DT = D // 128
KC = 3
CK = SK // KC
PAIRS = NH // 2
FF, NZ, RH, TOPK = 1024, 8, 64, 3
FT = FF // 128
EPS = 1e-5
MASKED = -1e15
WSCALE = 64.0
CHUNK = 1024
CHUNKS = 4
NCH = B * CHUNKS
R_USE, V_USE, X_USE, CTX_USE, Q_USE, K_USE, O_USE, X2_USE, FULL_USES = 1, 2, 4, 5, 7, 8, 10, 11, 11
LAST_O_USE, LAST_X2_USE = 4, 5
PREP_USES = 6


class Uses:

    def __init__(self, first, odd, shared):
        self.first, self.odd, self.shared = first, odd, shared

    def n(self, k):
        return self.first + k

    def bank(self, k):
        return self.shared[(self.odd + k) % 2]


class Steps:

    def __init__(self, eng, sem):
        self.eng, self.sem, self.base, self.n = eng, sem, 0, 0

    def begin(self, base):
        self.base, self.n = base, 0

    def done(self, ins):
        ins.then_inc(self.sem, 1)
        self.n += 1

    def link(self, ins):
        self.done(ins)
        self.eng.wait_ge(self.sem, self.base + self.n)


def flamingo_layer(nc, x, ctx, mask, g_xattn, g_ffn, Wq, bq, Wk, bk, Wv, bv, Wo, bo,
                   W1, b1, W2, b2, Wa, Wb, out):
    with ExitStack() as stack:
        def sb(name, shape, dt=F32):
            return stack.enter_context(nc.sbuf_tensor(name, shape, dt))

        def sem(name):
            return stack.enter_context(nc.semaphore(name))

        k_scr = nc.dram_tensor("k_scr", [B, DT, HD, 2, PAIRS, SK], F16).ap()
        q_scr = nc.dram_tensor("q_scr", [B, DT, HD, 4, PAIRS, SQ], F16).ap()
        r_scr = nc.dram_tensor("r_scr", [B, SQ, D], F32).ap()
        x2_scr = nc.dram_tensor("x2_scr", [B, 128, 2 * DT * SQ], F16).ap()

        wa = sb("wa", [128, NZ * 2 * DT * FF], F16)
        wb = sb("wb", [128, NZ * 2 * FT * D], F16)
        stage = sb("stage", [128, 2, CHUNK])
        wqkvo = sb("wqkvo", [128, 4, DT, D])
        bq_c = sb("bq_c", [128, DT])
        bk_c = sb("bk_c", [128, DT])
        bv_r = sb("bv_r", [128, D])
        bo_r = sb("bo_r", [128, D])
        w1_s = sb("w1_s", [128, DT, RH])
        w2_s = sb("w2_s", [RH, NZ])
        b1_c = sb("b1_c", [RH, 1])
        b2_r = sb("b2_r", [B, NZ])
        gates = sb("gates", [128, 2])
        tgate = sb("tgate", [128, 2])
        tf_w = sb("tf_w", [128, 1])
        ident = sb("ident", [128, 128])
        ident_b = sb("ident_b", [SQ, SQ], BF16)
        half = sb("half", [128, 1])
        ones = sb("ones", [B, 128])
        ctx_s = sb("ctx_s", [CK, KC, D])
        ctxT = sb("ctxT", [128, DT, SK])
        k_hl = sb("k_hl", [128, DT, 2, SK], F16)
        q_f = sb("q_f", [128, DT, SQ])
        q_hl = sb("q_hl", [128, DT, 2, 2, SQ], F16)
        kst = sb("kst", [128, 2, PAIRS * SK], F16)
        qst = sb("qst", [128, 2, PAIRS, SQ], F16)
        vpad = sb("vpad", [CK, KC, PAIRS, 64])
        probs = sb("probs", [SQ, 2, 2, SK])
        pT = sb("pT", [CK, 2, KC, 2 * SQ])
        mask_s = sb("mask_s", [SQ, SK], U8)
        maskb = sb("maskb", [SQ, 2, SK], BF16)
        xa = sb("xa", [SQ, D])
        xT = sb("xT", [128, DT * SQ])
        xr = sb("xr", [SQ, D])
        yo = sb("yo", [SQ, D])
        x2 = sb("x2", [SQ, D])
        res = sb("res", [SQ, D])
        x2T = sb("x2T", [128, 2, DT * SQ], F16)
        stat = sb("stat", [SQ, 6])
        mv = sb("mv", [SQ, 2])
        ve = sb("ve", [SQ, 1])
        rstd = sb("rstd", [SQ, 1])
        stat2 = sb("stat2", [SQ, 6])
        mv2 = sb("mv2", [SQ, 2])
        ve2 = sb("ve2", [SQ, 1])
        rstd2 = sb("rstd2", [SQ, 1])
        negmax = sb("negmax", [SQ, NH])
        rowsum = sb("rowsum", [SQ, 2, NH])
        rinv = sb("rinv", [SQ, NH])
        rexp = sb("rexp", [SQ, NH, HD])
        rT = sb("rT", [128, DT * SQ])
        oT = sb("oT", [128, DT * SQ])
        o_raw = sb("o_raw", [128, DT * SQ])
        pooled = sb("pooled", [128, DT, B])
        h_s = sb("h_s", [RH, B])
        lg = sb("lg", [B, NZ])
        top = sb("top", [B, NZ])
        nmx = sb("nmx", [B, 1])
        ez = sb("ez", [B, NZ])
        zs = sb("zs", [B, 1])
        zr = sb("zr", [B, 1])
        pz = sb("pz", [B, NZ])
        ptop = sb("ptop", [B, NZ])
        pidx = sb("pidx", [B, NZ], U32)
        ts = sb("ts", [B, 1])
        tr = sb("tr", [B, 1])
        wz = sb("wz", [B, TOPK])
        wdiag = sb("wdiag", [B, B, TOPK])
        wbc = sb("wbc", [128, B * TOPK])
        wcur = sb("wcur", [128, 2, TOPK])
        idx_row = sb("idx_row", [1, B * NZ], U32)
        x2b = sb("x2b", [128, 2, 2 * DT * SQ], F16)
        h_f = kst[:].rearrange("p a f -> p (a f)")[0:SQ, 0:2 * 2 * FF].bitcast(F32)
        hT = stage[:].rearrange("p a f -> p (a f)")[:, 0:2 * FT * SQ].bitcast(F16)
        rb = [xa[:], xr[:]]
        ob = [yo[:], x2[:]]

        bank = stack.enter_context(nc.psum_tensor("bank", [128, 8, 512], F32))
        flat = bank[:].rearrange("p a f -> p (a f)")
        PTB = 4 * 512
        OB = 256
        shared = [bank[:, 6, :], bank[:, 7, :]]

        def uses(b, par):
            if isinstance(b, int) and b == 0:
                return Uses(PREP_USES - 1, (PREP_USES - 1) % 2, shared)
            before_1 = PREP_USES - 1 + X2_USE - 2
            return Uses(before_1 + (b - 1) * FULL_USES, (before_1 + 1 + par) % 2, shared)

        names = ("wk_loaded wq_loaded wv_loaded wo_loaded bk_loaded bq_loaded const_loaded g_loaded ident_ready setup_pool setup_dve setup_act x_loaded ctx_loaded mask_loaded xr_loaded "
                 "k_written q_written k_stacked k_stacked2 q_stacked res_written x2_written "
                 "chunk_loaded0 chunk_loaded1 scaled hi_done lo_done "
                 "pe_s dve_max act_exp pe_t act_pt pe_pv act_o dve_o misc_full misc_free "
                 "khi_done klo_done qf_done qhi_done qlo_done kv_ready mask_ready ln1_var ln1_rstd xn_done xa_used ctx_used mask_used "
                 "vpad_ready rexp_done ot_done ln2_var ln2_rstd x2_done x2hi_done x2lo_done res_done xr_used pool_chain "
                 "h_full h_act lg_full e_done idx_done idx_loaded route_done wcur_done w_full "
                 "dve_passed pool_passed dve_step g1_done gelu_done ht_full hthi_done htlo_done g2_done y_done r_loaded x2b_loaded out_written").split()
        s = {n: sem(n) for n in names}
        chunk_loaded = [s["chunk_loaded0"], s["chunk_loaded1"]]

        def view_w(ap):
            return ap.rearrange("(t p) n -> p t n", p=128)

        block = stack.enter_context(nc.Block())

        def chunk_dst(z, c, hl):
            t = wa if c < 2 else wb
            return t[:, bass.ds(z * (4 * CHUNK) + hl * (2 * CHUNK) + (c % 2) * CHUNK, CHUNK)]

        def alone(eng, sem_, n, passed):
            eng.wait_ge(sem_, n)
            eng.sem_inc(passed, 1)

        def over_batches(eng, body):
            body(0, 0)
            with eng.Fori(0, (B - 2) // 2) as i:
                body(i * 2 + 1, 1)
                body(i * 2 + 2, 0)
            body(B - 1, 1)

        @block.sync
        def _(sp):
            for n in ("xr_used", "x2_written", "res_written", "y_done"):
                sp.sem_inc(s[n], 1)
            def load_prep(b):
                sp.dma_start(xa[:, :], x[bass.ds(b, 1), :, :].rearrange("o s d -> (o s) d")).then_inc(s["x_loaded"], 16)
                sp.dma_start(ctx_s[:, :, :], ctx[bass.ds(b, 1), :, :].rearrange("o (c r) d -> r (o c) d", r=CK)).then_inc(s["ctx_loaded"], 16)
                sp.dma_start(mask_s[:, :], mask[bass.ds(b, 1), :, :].rearrange("o s d -> (o s) d")).then_inc(s["mask_loaded"], 16)

            def stack_q(b):
                sp.wait_ge(s["qlo_done"], b + 1)
                for t in range(DT):
                    sp.dma_start(q_scr[bass.ds(b, 1), t, :, :, :, :].rearrange("o i a j f -> j (o i) a f"),
                                 q_hl[:, t, :, :, :].rearrange("p r a f -> p (r a) f")).then_inc(s["q_written"], 16)

            def stack_k(b, t):
                sp.wait_ge(s["klo_done"], b * 2 + t + 1)
                sp.dma_start(k_scr[bass.ds(b, 1), t, :, :, :, :].rearrange("o i a j f -> j (o i) a f"),
                             k_hl[:, t, :, :]).then_inc(s["k_written"], 16)

            def read_stacks(b, par):
                sp.wait_ge(s["q_written"], b * 32 + 32)
                run = PAIRS * SQ
                sp.dma_start(qst[:, par, :, :].rearrange("p a f -> p (a f)"),
                             bass.AP(q_scr.tensor, b * (DT * HD * 4 * run), [[run, 128], [1, run]])).then_inc(s["q_stacked"], 16)
                sp.wait_ge(s["k_written"], b * 32 + 32)
                run = PAIRS * SK
                for h in range(2):
                    sp.dma_start(kst[:, par, h * run // 2:(h + 1) * run // 2],
                                 bass.AP(k_scr.tensor, b * (DT * HD * 2 * run) + h * run // 2,
                                         [[run, DT * HD * 2], [0, 2], [1, run // 2]])).then_inc(s["k_stacked" if h == 0 else "k_stacked2"], 16)

            load_prep(0)
            sp.dma_start(wqkvo[:, 2, :, :], view_w(Wv)).then_inc(s["wv_loaded"], 16)
            stack_q(0)
            stack_k(0, 0)
            stack_k(0, 1)
            read_stacks(0, 0)
            sp.wait_ge(s["xa_used"], 1)
            sp.wait_ge(s["ctx_used"], 1)
            sp.wait_ge(s["mask_ready"], 1)
            load_prep(1)
            for t in range(DT):
                for j in range(4):
                    sp.dma_start(wqkvo[32 * j:32 * j + 32, 3, t, :], bass.AP(Wo.tensor, (4 * t + j) * HD * D,
                                 [[PAIRS * HD * D, 2], [D, HD], [1, D]])).then_inc(s["wo_loaded"], 16)

            def body(b, par):
                first = isinstance(b, int) and b == 0
                last = isinstance(b, int) and b == B - 1
                if not first:
                    sp.wait_ge(s["xr_used"], b)
                    sp.dma_start(xr[:, :], x[bass.ds(b - 1, 1), :, :].rearrange("o s d -> (o s) d")).then_inc(s["xr_loaded"], 16)
                if not last:
                    stack_q(b + 1)
                    stack_k(b + 1, 0)
                    stack_k(b + 1, 1)
                    read_stacks(b + 1, 1 - par)
                if not last:
                    sp.wait_ge(s["xa_used"], b + 2)
                    sp.wait_ge(s["ctx_used"], b + 2)
                    sp.wait_ge(s["mask_ready"], b + 2)
                    if isinstance(b, int):
                        if b + 2 < B:
                            load_prep(b + 2)
                    else:
                        load_prep(b + 2)
                if not first:
                    store_post(b - 1)

            def store_post(b):
                sp.wait_ge(s["res_done"], b + 1)
                sp.dma_start(r_scr[bass.ds(b, 1), :, :].rearrange("o s d -> (o s) d"), res[:, :]).then_inc(s["res_written"], 16)
                sp.wait_ge(s["x2lo_done"], b + 1)
                sp.dma_start(x2_scr[bass.ds(b, 1), :, :].rearrange("o p f -> (o p) f"),
                             x2T[:].rearrange("p a f -> p (a f)")).then_inc(s["x2_written"], 16)

            body(0, 0)
            with sp.Fori(0, (B - 4) // 2) as i:
                body(i * 2 + 1, 1)
                body(i * 2 + 2, 0)
            for b in range(B - 3, B):
                body(b, b % 2)
            sp.wait_ge(s["xr_used"], B)
            sp.dma_start(xr[:, :], x[B - 1, :, :]).then_inc(s["xr_loaded"], 16)
            store_post(B - 1)

            sp.wait_ge(s["idx_done"], 1)
            sp.dma_start(idx_row[:, :], pidx[:, :]).then_inc(s["idx_loaded"], 16)
            sp.wait_ge(s["res_written"], 16 * B + 1)
            sp.wait_ge(s["x2_written"], 16 * B + 1)

            def load_ffn(b, par):
                sp.dma_start(rb[par], r_scr[bass.ds(b, 1), :, :].rearrange("o s d -> (o s) d")).then_inc(s["r_loaded"], 16)
                sp.dma_start(x2b[:, par, :], x2_scr[bass.ds(b, 1), :, :].rearrange("o p f -> (o p) f")).then_inc(s["x2b_loaded"], 16)

            def store_out(b, par):
                sp.wait_ge(s["y_done"], b + 2)
                sp.dma_start(out[bass.ds(b, 1), :, :].rearrange("o s d -> (o s) d"), ob[par]).then_inc(s["out_written"], 16)

            load_ffn(0, 0)
            sp.wait_ge(s["r_loaded"], 16)
            sp.wait_ge(s["x2b_loaded"], 16)
            load_ffn(1, 1)
            with sp.Fori(0, (B - 2) // 2) as i:
                for par in range(2):
                    b = i * 2 + par
                    store_out(b, par)
                    sp.wait_ge(s["r_loaded"], b * 16 + 32)
                    sp.wait_ge(s["x2b_loaded"], b * 16 + 32)
                    load_ffn(b + 2, par)
            store_out(B - 2, 0)
            store_out(B - 1, 1)
            sp.wait_ge(s["out_written"], 16 * B)

        @block.gpsimd
        def _(pool):
            g = nc.gpsimd
            chain = Steps(pool, s["pool_chain"])
            def load_chunk(b, c):
                if c < 2:
                    src = Wa[bass.ds(b, 1), c * 128:(c + 1) * 128, :].rearrange("o p f -> (o p) f")
                    dst = stage[:, c % 2, :]
                else:
                    src = Wb[bass.ds(b, 1), (c - 2) * 512:(c - 1) * 512, :].rearrange("o (f p) n -> p (o f) n", p=128)
                    dst = stage[:, c % 2, :].rearrange("p (f n) -> p f n", n=D)
                g.dma_start(dst, src).then_inc(chunk_loaded[c % 2], 16)

            chain.link(g.memset(ident[:, :], 0.0))
            chain.link(g.affine_select(out=ident[:, :], in_=ident[:, :], compare_op=ALU.not_equal, fill=1.0,
                                       base=0, pattern=[[-1, 128]], channel_multiplier=1))
            pool.sem_inc(s["ident_ready"], 1)
            chain.link(g.tensor_copy(ident_b[:, :], ident[0:SQ, 0:SQ]))
            chain.link(g.memset(half[:, :], -0.5))
            chain.link(g.memset(ones[:, :], 1.0))
            def pow_rstd(dst, src, ready, n, signal):
                pool.wait_ge(ready, n)
                g.tensor_tensor(dst, src, half[0:SQ, :], ALU.pow).then_inc(signal, 1)

            load_chunk(0, 0)
            load_chunk(0, 1)
            pow_rstd(rstd[:, :], ve[:, :], s["ln1_var"], 1, s["ln1_rstd"])
            g.memset(vpad[:].rearrange("p a b c -> p (a b c)"), 0.0).then_inc(s["setup_pool"], 1)
            g.dma_start(bv_r[:, :], bass.AP(bv.tensor, 0, [[0, 128], [1, D]])).then_inc(s["const_loaded"], 16)
            g.dma_start(bo_r[:, :], bass.AP(bo.tensor, 0, [[0, 128], [1, D]])).then_inc(s["const_loaded"], 16)
            g.dma_start(w1_s[:, :, :], W1.rearrange("(t p) n -> p t n", p=128)).then_inc(s["const_loaded"], 16)
            g.dma_start(w2_s[:, :], W2).then_inc(s["const_loaded"], 16)
            g.dma_start(b1_c[:, :], b1.rearrange("(p o) -> p o", o=1), allow_slow_non_contiguous=True).then_inc(s["const_loaded"], 16)
            g.dma_start(b2_r[:, :], bass.AP(b2.tensor, 0, [[0, B], [1, NZ]])).then_inc(s["const_loaded"], 16)

            def scale_chunk(b, c):
                st = stage[:, c % 2, :]
                alone(pool, chunk_loaded[c % 2], b * 32 + 16 * (c // 2) + 16, s["pool_passed"])
                g.tensor_scalar(st, st, WSCALE, 1.0, ALU.mult, ALU.mult).then_inc(s["scaled"], 1)

            def lo_chunk(b, c):
                alone(pool, s["hi_done"], b * CHUNKS + c + 1, s["pool_passed"])
                g.tensor_tensor(chunk_dst(b, c, 1), stage[:, c % 2, :], chunk_dst(b, c, 0), ALU.subtract).then_inc(s["lo_done"], 1)

            def reload(b, c):
                alone(pool, s["lo_done"], b * CHUNKS + c - 1, s["pool_passed"])
                load_chunk(b, c)

            def body(b, par):
                first = isinstance(b, int) and b == 0
                last = isinstance(b, int) and b == B - 1
                if not last:
                    pow_rstd(rstd[:, :], ve[:, :], s["ln1_var"], b + 2, s["ln1_rstd"])
                if not first:
                    lo_chunk(b - 1, CHUNKS - 1)
                    reload(b, 1)
                scale_chunk(b, 0)
                scale_chunk(b, 1)
                lo_chunk(b, 0)
                reload(b, 2)
                lo_chunk(b, 1)
                if not first:
                    pow_rstd(rstd2[:, :], ve2[:, :], s["ln2_var"], b, s["ln2_rstd"])
                reload(b, 3)
                scale_chunk(b, 2)
                scale_chunk(b, 3)
                lo_chunk(b, 2)
                if not last:
                    reload(b + 1, 0)

            over_batches(pool, body)
            lo_chunk(B - 1, CHUNKS - 1)
            pow_rstd(rstd2[:, :], ve2[:, :], s["ln2_var"], B, s["ln2_rstd"])

        @block.scalar
        def _(act):
            a = nc.scalar
            for n, w, name in ((0, Wq, "wq_loaded"), (1, Wk, "wk_loaded")):
                a.dma_start(wqkvo[:, n, :, :], view_w(w)).then_inc(s[name], 16)
            a.dma_start(bk_c[:, :], bk.rearrange("(t p) -> p t", p=128), allow_slow_non_contiguous=True).then_inc(s["bk_loaded"], 16)
            a.dma_start(bq_c[:, :], bq.rearrange("(t p) -> p t", p=128), allow_slow_non_contiguous=True).then_inc(s["bq_loaded"], 16)
            a.dma_start(gates[:, 0:1], bass.AP(g_xattn.tensor, 0, [[0, 128], [1, 1]])).then_inc(s["g_loaded"], 16)
            a.dma_start(gates[:, 1:2], bass.AP(g_ffn.tensor, 0, [[0, 128], [1, 1]])).then_inc(s["g_loaded"], 16)
            act.wait_ge(s["g_loaded"], 32)
            a.activation(tgate[:, :], gates[:, :], ACT.Tanh).then_inc(s["setup_act"], 1)

            def exp_head(b, par, p, e):
                if e == 0:
                    act.wait_ge(s["dve_max"], b * PAIRS + p + 1)
                    if not (isinstance(b, int) and b == 0 and p < 2):
                        act.wait_ge(s["pe_t"], b * PAIRS + p - 1)
                h = 2 * p + e
                a.activation(probs[:, p % 2, e, :], bank[0:SQ, 2 * (p % 2) + e, 0:SK], ACT.Exp,
                             bias=negmax[:, h:h + 1], accum_out=rowsum[:, par, h:h + 1]).then_inc(s["act_exp"], 1)

            def pt_copy(b, p):
                act.wait_ge(s["pe_t"], b * PAIRS + p + 1)
                if not (isinstance(b, int) and b == 0 and p < 2):
                    act.wait_ge(s["pe_pv"], b * PAIRS + p - 1)
                a.activation(pT[:, p % 2, :, :], flat[0:CK, PTB:PTB + KC * 256].rearrange("p (c f) -> p c f", c=KC)[:, :, 0:2 * SQ],
                             ACT.Copy).then_inc(s["act_pt"], 1)

            def o_copy(b):
                act.wait_ge(s["pe_pv"], b * PAIRS + PAIRS)
                if not (isinstance(b, int) and b == 0):
                    act.wait_ge(s["dve_o"], b)
                a.activation(o_raw[:, :], flat[:, PTB + 512 + OB:PTB + 512 + OB + DT * SQ], ACT.Copy).then_inc(s["act_o"], 1)

            def k_hi(b, t, u, k):
                act.wait_ge(s["misc_full"], u.n(k))
                if not (isinstance(b, int) and b == 0):
                    act.wait_ge(s["k_written"], b * 32)
                a.activation(k_hl[:, t, 0, :], u.bank(k)[:, 0:SK], ACT.Identity, bias=bk_c[:, t:t + 1]).then_inc(s["khi_done"], 1)

            def q_hi(b):
                act.wait_ge(s["qf_done"], b + 1)
                if not (isinstance(b, int) and b == 0):
                    act.wait_ge(s["q_written"], b * 32)
                a.activation(q_hl[:, :, :, 0, :], bass.AP(q_f, 0, [[DT * SQ, 128], [SQ, DT], [0, 2], [1, SQ]]), ACT.Copy).then_inc(s["qhi_done"], 1)

            def x2_hi(b, u, k):
                act.wait_ge(s["misc_full"], u.n(k))
                if not (isinstance(b, int) and b == 0):
                    act.wait_ge(s["x2_written"], b * 16 + 1)
                a.activation(x2T[:, 0, :], u.bank(k)[:, 0:DT * SQ], ACT.Copy).then_inc(s["x2hi_done"], 1)

            prep_u = Uses(0, 0, shared)
            act.wait_ge(s["bk_loaded"], 16)
            q_hi(0)
            k_hi(0, 0, prep_u, 5)
            k_hi(0, 1, prep_u, 6)
            exp_head(0, 0, 0, 0)
            exp_head(0, 0, 0, 1)
            exp_head(0, 0, 1, 0)

            def body(b, par):
                first = isinstance(b, int) and b == 0
                last = isinstance(b, int) and b == B - 1
                u = uses(b, par)

                def exps(p, e):
                    if p < PAIRS:
                        exp_head(b, par, p, e)
                    elif not last:
                        exp_head(b + 1, 1 - par, p - PAIRS, e)

                for p in range(PAIRS):
                    pt_copy(b, p)
                    if p == 0 and not first:
                        o_copy(b - 1)
                    exps(p + 1, 1)
                    if p == 2 and not last:
                        k_hi(b + 1, 0, u, K_USE)
                    if p == 6 and not first:
                        x2_hi(b - 1, u, X2_USE if not last else LAST_X2_USE)
                    exps(p + 2, 0)
                    if p == 1 and not last:
                        q_hi(b + 1)
                    if p == 2 and not last:
                        k_hi(b + 1, 1, u, K_USE + 1)

            over_batches(act, body)
            o_copy(B - 1)
            x2_hi(B - 1, uses(B - 1, 1), LAST_X2_USE + 3)
            act.wait_ge(s["const_loaded"], 96)
            act.wait_ge(s["h_full"], 1)
            a.activation(h_s[:, :], shared[0][0:RH, 0:B], ACT.Tanh, bias=b1_c[:, :], scale=1.0 / SQ).then_inc(s["h_act"], 1)
            act.wait_ge(s["lg_full"], 2)
            a.activation(ez[:, :], lg[:, :], ACT.Exp, bias=nmx[:, :], accum_out=zs[:, :]).then_inc(s["e_done"], 1)
            act.wait_ge(s["route_done"], 1)

            def gelu(u_done, hf):
                act.wait_ge(s["g1_done"], u_done * 2 + hf + 1)
                act.wait_ge(s["ht_full"], u_done * 2)
                a.activation(h_f[:, hf * 512:(hf + 1) * 512], bank[0:SQ, hf, :], ACT.Gelu_apprx_tanh,
                             scale=1.0 / WSCALE).then_inc(s["gelu_done"], 1)

            def ht_hi(b, par, k, hf):
                u = b * TOPK + k
                if k == 0 and hf == 0:
                    act.wait_ge(s["wcur_done"], b + 1)
                act.wait_ge(s["ht_full"], u * 2 + hf + 1)
                if not (isinstance(u, int) and u == 0):
                    act.wait_ge(s["g2_done"], u)
                a.activation(hT[:, hf * 448:hf * 448 + 448], bank[:, 2 + hf, 0:448], ACT.Copy,
                             scale=wcur[:, par, k:k + 1]).then_inc(s["hthi_done"], 1)

            def ffn_body(b, par, last):
                for k in range(TOPK):
                    u = b * TOPK + k
                    for hf in range(2):
                        ht_hi(b, par, k, hf)
                        if not (last and k == TOPK - 1):
                            gelu(u + 1, hf)

            gelu(0, 0)
            gelu(0, 1)
            ffn_body(0, 0, False)
            with act.Fori(0, (B - 2) // 2) as i:
                ffn_body(i * 2 + 1, 1, False)
                ffn_body(i * 2 + 2, 0, False)
            ffn_body(B - 1, 1, True)

        N_MAX, N_V, N_PREP, N_POST = PAIRS, 3, 0, 0

        @block.vector
        def _(dve):
            v = nc.vector
            st = Steps(dve, s["dve_step"])
            tot = [0]
            def mask_bias(b, par):
                dve.wait_ge(s["mask_loaded"], b * 16 + 16)
                if not (isinstance(b, int) and b < 2):
                    dve.wait_ge(s["pe_s"], b * PAIRS - PAIRS)
                v.tensor_scalar(maskb[:, par, :], mask_s[:, :], MASKED, 1.0, ALU.mult, ALU.mult).then_inc(s["mask_ready"], 1)

            def row_max(b, p):
                dve.wait_ge(s["pe_s"], b * PAIRS + p + 1)
                v.tensor_reduce(negmax[:, 2 * p:2 * p + 2], bank[0:SQ, 2 * (p % 2):2 * (p % 2) + 2, 0:SK], AX.X, ALU.max,
                                negate=True).then_inc(s["dve_max"], 1)

            def full(u, k):
                dve.wait_ge(s["misc_full"], u.n(k))

            def layernorm_stats(src, stat_, mv_, ve_, ready):
                st.link(v.bn_stats(stat_[:, :], src))
                dve.sem_inc(s["dve_passed"], 1)
                st.link(v.bn_aggr(mv_[:, :], stat_[:, :]))
                v.tensor_scalar(ve_[:, :], mv_[:, 1:2], EPS, None, ALU.add).then_inc(ready, 1)

            def ln1_stats(b):
                dve.wait_ge(s["x_loaded"], b * 16 + 16)
                layernorm_stats(xa[:, :], stat, mv, ve, s["ln1_var"])

            def ln1_apply(b):
                dve.wait_ge(s["ln1_rstd"], b + 1)
                v.tensor_scalar(xa[:, :], xa[:, :], mv[:, 0:1], rstd[:, :], ALU.subtract, ALU.mult).then_inc(s["xn_done"], 1)

            def ctx_copy(t, u, k):
                full(u, k)
                if t == DT - 1:
                    dve.sem_inc(s["ctx_used"], 1)
                v.tensor_copy(ctxT[:, t, :], u.bank(k)[:, 0:SK]).then_inc(s["misc_free"], 1)

            def x_copy(u, k):
                full(u, k)
                dve.sem_inc(s["xa_used"], 1)
                v.tensor_copy(xT[:, :], u.bank(k)[:, 0:DT * SQ]).then_inc(s["misc_free"], 1)

            def k_lo(b, t, u, k):
                dve.wait_ge(s["khi_done"], b * 2 + t + 1)
                v.scalar_tensor_tensor(out=k_hl[:, t, 1, :], in0=u.bank(k)[:, 0:SK], scalar=bk_c[:, t:t + 1],
                                       in1=k_hl[:, t, 0, :], op0=ALU.add, op1=ALU.subtract).then_inc(s["klo_done"], 1)
                dve.wait_ge(s["klo_done"], b * 2 + t + 1)
                dve.sem_inc(s["misc_free"], 1)

            def q_full(b, u, k):
                full(u, k)
                if not (isinstance(b, int) and b == 0):
                    dve.wait_ge(s["q_written"], b * 32)
                for t in range(DT):
                    ins = v.tensor_scalar(q_f[:, t, :], u.bank(k)[:, t * SQ:(t + 1) * SQ], bq_c[:, t:t + 1], HD ** -0.5,
                                          ALU.add, ALU.mult)
                    if t == 0:
                        st.done(ins)
                ins.then_inc(s["qf_done"], 1)
                dve.wait_ge(s["qf_done"], b + 1)
                dve.sem_inc(s["misc_free"], 1)

            def q_lo(b):
                dve.wait_ge(s["qhi_done"], b + 1)
                v.tensor_tensor(q_hl[:, :, :, 1, :], bass.AP(q_f, 0, [[DT * SQ, 128], [SQ, DT], [0, 2], [1, SQ]]),
                                q_hl[:, :, :, 0, :], ALU.subtract).then_inc(s["qlo_done"], 1)

            def v_copy(c, src):
                out_ = bass.AP(vpad, c * PAIRS * 64, [[KC * PAIRS * 64, CK], [64, PAIRS], [48, 2], [1, HD]])
                return v.tensor_tensor(out_, src.rearrange("p (e q i) -> p q e i", e=2, i=HD),
                                       bv_r[0:CK, :].rearrange("p (e q i) -> p q e i", e=2, i=HD), ALU.add)

            def v_stage(b, u, first):
                if not (isinstance(b, int) and b == 0):
                    dve.wait_ge(s["pe_pv"], b * PAIRS)
                full(u, V_USE)
                st.done(v_copy(0, u.bank(V_USE)[0:CK, 0:D]))
                v_copy(1, u.bank(V_USE)[0:CK, D:2 * D]).then_inc(s["misc_free"], 1)
                if not first:
                    o_scale(b - 1)
                full(u, V_USE + 1)
                v_copy(2, u.bank(V_USE + 1)[0:CK, 0:D]).then_inc(s["misc_free"], 1)
                dve.wait_ge(s["dve_step"], st.base + st.n)
                dve.wait_ge(s["misc_free"], u.n(V_USE + 1))
                dve.sem_inc(s["vpad_ready"], 1)

            def row_sums(b, par):
                dve.wait_ge(s["act_exp"], b * NH + NH)
                st.link(v.reciprocal(rinv[:, :], rowsum[:, par, :]))
                v.tensor_copy(rexp[:, :, :], bass.AP(rinv, 0, [[NH, SQ], [1, NH], [0, HD]])).then_inc(s["rexp_done"], 1)

            def rt_copy(u, k):
                full(u, k)
                v.tensor_copy(rT[:, :], u.bank(k)[:, 0:DT * SQ]).then_inc(s["misc_free"], 1)
                dve.wait_ge(s["misc_free"], u.n(k))

            def o_scale(b):
                dve.wait_ge(s["act_o"], b + 1)
                v.tensor_tensor(oT[:, :], o_raw[:, :], rT[:, :], ALU.mult).then_inc(s["dve_o"], 1)

            def residual(b, u, k):
                full(u, k)
                v.tensor_tensor(yo[:, :], u.bank(k)[0:SQ, 0:D], bo_r[0:SQ, :], ALU.add).then_inc(s["misc_free"], 1)
                dve.wait_ge(s["misc_free"], u.n(k))
                dve.wait_ge(s["xr_loaded"], b * 16 + 16)
                st.link(v.scalar_tensor_tensor(out=xr[:, :], in0=yo[:, :], scalar=tgate[0:SQ, 0:1], in1=xr[:, :], op0=ALU.mult, op1=ALU.add))
                layernorm_stats(xr[:, :], stat2, mv2, ve2, s["ln2_var"])

            def ln2_apply(b):
                dve.wait_ge(s["ln2_rstd"], b + 1)
                v.tensor_scalar(x2[:, :], xr[:, :], mv2[:, 0:1], rstd2[:, :], ALU.subtract, ALU.mult).then_inc(s["x2_done"], 1)
                dve.wait_ge(s["x2_done"], b + 1)
                if not (isinstance(b, int) and b == 0):
                    dve.wait_ge(s["res_written"], b * 16 + 1)
                v.scalar_tensor_tensor(out=res[:, :], in0=x2[:, :], scalar=tgate[0:SQ, 1:2], in1=xr[:, :], op0=ALU.mult,
                                       op1=ALU.add).then_inc(s["res_done"], 1)
                dve.wait_ge(s["res_done"], b + 1)
                dve.sem_inc(s["xr_used"], 1)

            def x2_lo(b, u, k):
                dve.wait_ge(s["x2hi_done"], b + 1)
                src = u.bank(k)[:, 0:DT * SQ]
                v.tensor_tensor(x2T[:, 1, :], src, x2T[:, 0, :], ALU.subtract).then_inc(s["x2lo_done"], 1)
                dve.wait_ge(s["x2lo_done"], b + 1)
                v.tensor_reduce(pooled[:, :, bass.ds(b, 1)], src.rearrange("p (t f) -> p t f", t=DT), AX.X,
                                ALU.add).then_inc(s["misc_free"], 1)

            def w_hi(b, c):
                alone(dve, s["scaled"], b * CHUNKS + c + 1, s["dve_passed"])
                v.tensor_copy(chunk_dst(b, c, 0), stage[:, c % 2, :]).then_inc(s["hi_done"], 1)

            prep_u = Uses(0, 0, shared)
            ln1_stats(0)
            ln1_apply(0)
            x_copy(prep_u, 1)
            ctx_copy(0, prep_u, 2)
            ctx_copy(1, prep_u, 3)
            dve.wait_ge(s["bq_loaded"], 16)
            q_full(0, prep_u, 4)
            q_lo(0)
            dve.wait_ge(s["bk_loaded"], 16)
            k_lo(0, 0, prep_u, 5)
            k_lo(0, 1, prep_u, 6)
            mask_bias(0, 0)
            dve.wait_ge(s["setup_act"], 1)
            v.tensor_scalar(tf_w[:, :], tgate[:, 1:2], 1.0 / WSCALE, None, ALU.mult).then_inc(s["setup_dve"], 1)
            row_max(0, 0)
            row_max(0, 1)
            dve.wait_ge(s["const_loaded"], 96)
            dve.wait_ge(s["setup_pool"], 1)
            SET = st.n
            counts = {}
            W_SLOTS = (3, 7)

            def body(b, par):
                first = isinstance(b, int) and b == 0
                last = isinstance(b, int) and b == B - 1
                st.begin(SET if first else SET + FIRST + FULL * (b - 1))
                u = uses(b, par)
                for p in range(PAIRS):
                    if p == 0:
                        if not last:
                            ln1_stats(b + 1)
                        if not first:
                            rt_copy(u, R_USE)
                            w_hi(b - 1, 3)
                        v_stage(b, u, first)
                    if p == 1 and not last:
                        x_copy(u, X_USE)
                        ctx_copy(0, u, CTX_USE)
                    if p == 2:
                        if not last:
                            q_lo(b + 1)
                        w_hi(b, 0)
                    if p == 3 and not last:
                        k_lo(b + 1, 1, u, K_USE + 1)
                    if p < PAIRS - 2:
                        row_max(b, p + 2)
                    elif not last:
                        row_max(b + 1, p - PAIRS + 2)
                    if p == 0 and not last:
                        ln1_apply(b + 1)
                    if p == 1 and not last:
                        ctx_copy(1, u, CTX_USE + 1)
                        q_full(b + 1, u, Q_USE)
                    if p == 2 and not last:
                        k_lo(b + 1, 0, u, K_USE)
                    if p == 3 and not last:
                        mask_bias(b + 1, 1 - par)
                    if p == 4 and not first:
                        residual(b - 1, u, LAST_O_USE if last else O_USE)
                    if p == 5 and not first:
                        ln2_apply(b - 1)
                    if p == 6:
                        row_sums(b, par)
                        if not first:
                            x2_lo(b - 1, u, LAST_X2_USE if last else X2_USE)
                    if p in W_SLOTS:
                        w_hi(b, 1 + W_SLOTS.index(p))
                counts["last" if last else "first" if first else "full"] = st.n

            FIRST, FULL = 5, 8
            over_batches(dve, body)
            assert counts["first"] == FIRST and counts["full"] == FULL, counts
            st.begin(SET + FIRST + FULL * (B - 2) + counts["last"])
            u = uses(B - 1, 1)
            rt_copy(u, LAST_X2_USE + 1)
            w_hi(B - 1, 3)
            o_scale(B - 1)
            residual(B - 1, u, LAST_X2_USE + 2)
            ln2_apply(B - 1)
            x2_lo(B - 1, u, LAST_X2_USE + 3)

            dve.wait_ge(s["lg_full"], 1)
            st.link(v.tensor_tensor(lg[:, :], shared[0][0:B, 0:NZ], b2_r[:, :], ALU.add))
            st.link(v.max(top[:, :], lg[:, :]))
            v.tensor_scalar(nmx[:, :], top[:, 0:1], -1.0, None, ALU.mult).then_inc(s["lg_full"], 1)
            dve.wait_ge(s["e_done"], 1)
            st.link(v.reciprocal(zr[:, :], zs[:, :]))
            st.link(v.tensor_scalar(pz[:, :], ez[:, :], zr[:, :], None, ALU.mult))
            st.link(v.max(ptop[:, :], pz[:, :]))
            v.max_index(pidx[:, :], ptop[:, :], pz[:, :]).then_inc(s["idx_done"], 1)
            st.link(v.tensor_reduce(ts[:, :], ptop[:, 0:TOPK], AX.X, ALU.add))
            st.link(v.reciprocal(tr[:, :], ts[:, :]))
            st.link(v.tensor_scalar(wz[:, :], ptop[:, 0:TOPK], tr[:, :], None, ALU.mult))
            v.tensor_tensor(wdiag[:, :, :], bass.AP(wz, 0, [[TOPK, B], [0, B], [1, TOPK]]),
                            bass.AP(ident, 0, [[128, B], [1, B], [0, TOPK]]), ALU.mult).then_inc(s["w_full"], 1)
            dve.wait_ge(s["w_full"], 2)
            v.tensor_copy(wbc[:, :], shared[0][:, 0:B * TOPK]).then_inc(s["route_done"], 1)
            dve.wait_ge(s["route_done"], 1)
            dve.wait_ge(s["setup_dve"], 1)

            def ffn_body(b, par):
                v.tensor_copy(wcur[:, par, :], wbc[:, bass.ds(b * TOPK, TOPK)]).then_inc(s["wcur_done"], 1)
                dve.wait_ge(s["wcur_done"], b + 1)
                for k in range(TOPK):
                    u = b * TOPK + k
                    for hf in range(2):
                        dve.wait_ge(s["hthi_done"], u * 2 + hf + 1)
                        v.scalar_tensor_tensor(out=hT[:, FT * SQ + hf * 448:FT * SQ + hf * 448 + 448], in0=bank[:, 2 + hf, 0:448],
                                               scalar=wcur[:, par, k:k + 1], in1=hT[:, hf * 448:hf * 448 + 448],
                                               op0=ALU.mult, op1=ALU.subtract).then_inc(s["htlo_done"], 1)
                dve.wait_ge(s["g2_done"], b * TOPK + TOPK)
                dve.wait_ge(s["r_loaded"], b * 16 + 16)
                if not isinstance(b, int):
                    dve.wait_ge(s["out_written"], b * 16 - 16)
                v.scalar_tensor_tensor(out=ob[par], in0=bank[0:SQ, 4 + par, 0:D], scalar=tf_w[0:SQ, :], in1=rb[par],
                                       op0=ALU.mult, op1=ALU.add).then_inc(s["y_done"], 1)

            ffn_body(0, 0)
            ffn_body(1, 1)
            with dve.Fori(0, (B - 2) // 2) as i:
                for par in range(2):
                    b = i * 2 + 2 + par
                    ffn_body(b, par)

        @block.tensor
        def _(pe):
            T = nc.tensor
            wq_s, wk_s, wv_s, wo_s = (wqkvo[:, n, :, :] for n in range(4))
            pe.wait_ge(s["ident_ready"], 1)

            def use(u, k, reads=-2):
                n = max(k - 2, reads)
                if not (isinstance(u.first, int) and u.n(n) <= 0):
                    pe.wait_ge(s["misc_free"], u.n(n))
                return u.bank(k)

            def full(ins):
                ins.then_inc(s["misc_full"], 1)

            def scores(b, par, p):
                if p == 0:
                    pe.wait_ge(s["k_stacked"], b * 16 + 16)
                    pe.wait_ge(s["q_stacked"], b * 16 + 16)
                    pe.wait_ge(s["mask_ready"], b + 1)
                if p == PAIRS // 2:
                    pe.wait_ge(s["k_stacked2"], b * 16 + 16)
                if not (isinstance(b, int) and b == 0 and p < 2):
                    pe.wait_ge(s["act_exp"], b * NH + 2 * p - 2)
                for e in range(2):
                    o = bank[0:SQ, 2 * (p % 2) + e, 0:SK]
                    T.matmul(o, ident_b[:, :], maskb[:, par, :], start=True, stop=False)
                for e in range(2):
                    o = bank[0:SQ, 2 * (p % 2) + e, 0:SK]
                    ins = T.matmul(o, qst[64 * e:64 * e + 64, par, p, :], kst[64 * e:64 * e + 64, par, p * SK:(p + 1) * SK],
                                   start=False, stop=True)
                ins.then_inc(s["pe_s"], 1)

            def transpose_probs(b, p):
                for e in range(2):
                    pe.wait_ge(s["act_exp"], b * NH + 2 * p + e + 1)
                    for c in range(KC):
                        o = PTB + c * 256 + e * SQ
                        ins = T.transpose(flat[0:CK, o:o + SQ], probs[:, p % 2, e, c * CK:(c + 1) * CK], ident[0:SQ, 0:SQ])
                ins.then_inc(s["pe_t"], 1)

            def pv(b, p):
                t, j = p // 4, p % 4
                pe.wait_ge(s["act_pt"], b * PAIRS + p + 1)
                if p == 0:
                    pe.wait_ge(s["vpad_ready"], b + 1)
                    if not (isinstance(b, int) and b == 0):
                        pe.wait_ge(s["act_o"], b)
                o = flat[32 * j:32 * j + 32, PTB + 512 + OB + t * SQ:PTB + 512 + OB + (t + 1) * SQ]
                for e in range(2):
                    for c in range(KC):
                        ins = T.matmul(o, vpad[:, c, p, 32 * e:32 * e + 32], pT[:, p % 2, c, e * SQ:(e + 1) * SQ],
                                       start=(e == 0 and c == 0), stop=(e == 1 and c == KC - 1))
                ins.then_inc(s["pe_pv"], 1)

            def ctx_t(b, t, u, k):
                m = use(u, k)
                if t == 0:
                    pe.wait_ge(s["ctx_loaded"], b * 16 + 16)
                for c in range(KC):
                    ins = T.transpose(m[:, c * CK:(c + 1) * CK], ctx_s[:, c, t * 128:(t + 1) * 128], ident[0:CK, 0:CK])
                full(ins)

            def k_proj(t, u, k, ctx_use):
                m = use(u, k, ctx_use)
                for kt in range(DT):
                    ins = T.matmul(m[:, 0:SK], wk_s[:, kt, t * 128:(t + 1) * 128], ctxT[:, kt, :], start=(kt == 0), stop=(kt == DT - 1))
                full(ins)

            def x_t(b, u, k):
                pe.wait_ge(s["xn_done"], b + 1)
                m = use(u, k)
                for t in range(DT):
                    ins = T.transpose(m[:, t * SQ:(t + 1) * SQ], xa[:, t * 128:(t + 1) * 128], ident[0:SQ, 0:SQ])
                full(ins)

            def q_proj(u, k, x_use):
                m = use(u, k, x_use)
                for t in range(DT):
                    for kt in range(DT):
                        ins = T.matmul(m[:, t * SQ:(t + 1) * SQ], wq_s[:, kt, t * 128:(t + 1) * 128], xT[:, kt * SQ:(kt + 1) * SQ],
                                       start=(kt == 0), stop=(kt == DT - 1))
                full(ins)

            def v_proj(u):
                for k, cs in ((V_USE, (0, 1)), (V_USE + 1, (2,))):
                    m = use(u, k)
                    for c in cs:
                        for kt in range(DT):
                            ins = T.matmul(m[0:CK, (c % 2) * D:(c % 2 + 1) * D], ctxT[:, kt, c * CK:(c + 1) * CK], wv_s[:, kt, :],
                                           start=(kt == 0), stop=(kt == DT - 1))
                    full(ins)

            def r_t(b, u, k):
                pe.wait_ge(s["rexp_done"], b + 1)
                m = use(u, k)
                for t in range(DT):
                    ins = T.transpose(m[:, t * SQ:(t + 1) * SQ], rexp[:].rearrange("p h i -> p (h i)")[:, t * 128:(t + 1) * 128],
                                      ident[0:SQ, 0:SQ])
                full(ins)

            def o_proj(b, u, k):
                pe.wait_ge(s["dve_o"], b + 1)
                m = use(u, k)
                for t in range(DT):
                    ins = T.matmul(m[0:SQ, 0:D], oT[:, t * SQ:(t + 1) * SQ], wo_s[:, t, :], start=(t == 0), stop=(t == DT - 1))
                full(ins)

            def x2_t(b, u, k):
                pe.wait_ge(s["x2_done"], b + 1)
                m = use(u, k)
                for t in range(DT):
                    ins = T.transpose(m[:, t * SQ:(t + 1) * SQ], x2[:, t * 128:(t + 1) * 128], ident[0:SQ, 0:SQ])
                full(ins)

            prep_u = Uses(0, 0, shared)
            x_t(0, prep_u, 1)
            ctx_t(0, 0, prep_u, 2)
            ctx_t(0, 1, prep_u, 3)
            pe.wait_ge(s["wq_loaded"], 16)
            q_proj(prep_u, 4, 1)
            pe.wait_ge(s["wk_loaded"], 16)
            k_proj(0, prep_u, 5, 3)
            k_proj(1, prep_u, 6, 3)
            pe.wait_ge(s["setup_pool"], 1)
            scores(0, 0, 0)
            scores(0, 0, 1)
            pe.wait_ge(s["wv_loaded"], 16)

            def body(b, par):
                first = isinstance(b, int) and b == 0
                last = isinstance(b, int) and b == B - 1
                u = uses(b, par)
                for p in range(PAIRS):
                    if p > 0:
                        pv(b, p - 1)
                    elif not first:
                        pv(b - 1, PAIRS - 1)
                    transpose_probs(b, p)
                    if p == 0 and not first:
                        r_t(b - 1, u, R_USE)
                    if not last:
                        if p == 1:
                            x_t(b + 1, u, X_USE)
                            ctx_t(b + 1, 0, u, CTX_USE)
                        if p == 2:
                            k_proj(0, u, K_USE, CTX_USE + 1)
                    if p == 0:
                        v_proj(u)
                    if p < PAIRS - 2:
                        scores(b, par, p + 2)
                    elif not last:
                        scores(b + 1, 1 - par, p - PAIRS + 2)
                    if not last:
                        if p == 1:
                            ctx_t(b + 1, 1, u, CTX_USE + 1)
                            q_proj(u, Q_USE, X_USE)
                        if p == 2:
                            k_proj(1, u, K_USE + 1, CTX_USE + 1)
                    if p == 3 and not first:
                        o_proj(b - 1, u, LAST_O_USE if last else O_USE)
                    if p == 6 and not first:
                        x2_t(b - 1, u, LAST_X2_USE if last else X2_USE)
                if first:
                    pe.wait_ge(s["wo_loaded"], DT * 4 * 16)

            over_batches(pe, body)
            u = uses(B - 1, 1)
            pv(B - 1, PAIRS - 1)
            r_t(B - 1, u, LAST_X2_USE + 1)
            o_proj(B - 1, u, LAST_X2_USE + 2)
            x2_t(B - 1, u, LAST_X2_USE + 3)

            pe.wait_ge(s["const_loaded"], 96)
            pe.wait_ge(s["misc_free"], u.n(LAST_X2_USE + 3))
            for t in range(DT):
                ins = T.matmul(shared[0][0:RH, 0:B], w1_s[:, t, :], pooled[:, t, :], start=(t == 0), stop=(t == DT - 1))
            ins.then_inc(s["h_full"], 1)
            pe.wait_ge(s["h_act"], 1)
            T.matmul(shared[0][0:B, 0:NZ], h_s[:, :], w2_s[:, :], start=True, stop=True).then_inc(s["lg_full"], 1)
            pe.wait_ge(s["w_full"], 1)
            T.matmul(shared[0][:, 0:B * TOPK], ones[:, :], wdiag[:].rearrange("p a b -> p (a b)"), start=True, stop=True).then_inc(s["w_full"], 1)
            pe.wait_ge(s["idx_loaded"], 16)
            pe.wait_ge(s["hi_done"], NCH)
            pe.wait_ge(s["lo_done"], NCH)

            def zone(b, k):
                return pe.value_load(idx_row[0:1, bass.ds(b * NZ + k, 1)], min_val=0, max_val=NZ - 1)

            def g1(b, par, k, e, hf):
                u = b * TOPK + k
                if k == 0 and hf == 0:
                    pe.wait_ge(s["x2b_loaded"], b * 16 + 16)
                if not (isinstance(u, int) and u == 0):
                    pe.wait_ge(s["gelu_done"], u * 2 - 1 + hf)
                o = bank[0:SQ, hf, :]
                n = 0
                for t in range(DT):
                    for xs, ws in ((0, 0), (0, 1), (1, 0)):
                        ins = T.matmul(o, x2b[:, par, xs * DT * SQ + t * SQ:xs * DT * SQ + (t + 1) * SQ],
                                       wa[:, bass.ds(e * (4 * CHUNK) + ws * (2 * CHUNK) + t * CHUNK + hf * 512, 512)],
                                       start=(n == 0), stop=(n == 3 * DT - 1))
                        n += 1
                ins.then_inc(s["g1_done"], 1)

            def ht(b, k, hf):
                u = b * TOPK + k
                pe.wait_ge(s["gelu_done"], u * 2 + hf + 1)
                if not (isinstance(u, int) and u == 0):
                    pe.wait_ge(s["htlo_done"], u * 2 - 1 + hf)
                for f in range(4):
                    ins = T.transpose(bank[:, 2 + hf, f * SQ:(f + 1) * SQ], h_f[:, hf * 512 + f * 128:hf * 512 + (f + 1) * 128],
                                      ident[0:SQ, 0:SQ])
                ins.then_inc(s["ht_full"], 1)

            def g2(b, par, k, e):
                u = b * TOPK + k
                if k == 0 and not (isinstance(b, int) and b < 2):
                    pe.wait_ge(s["y_done"], b)
                o = bank[0:SQ, 4 + par, 0:D]
                for f in range(FT):
                    if f % 4 == 0:
                        pe.wait_ge(s["htlo_done"], u * 2 + f // 4 + 1)
                    for hs, ws in ((0, 0), (0, 1), (1, 0)):
                        ins = T.matmul(o, hT[:, hs * FT * SQ + f * SQ:hs * FT * SQ + (f + 1) * SQ],
                                       wb[:, bass.ds(e * (4 * CHUNK) + ws * (2 * CHUNK) + f * D, D)],
                                       start=(k == 0 and f == 0 and hs == 0 and ws == 0), stop=(k == TOPK - 1 and f == FT - 1 and hs == 1))
                ins.then_inc(s["g2_done"], 1)

            def ffn_body(b, par, last):
                e = None
                for k in range(TOPK):
                    if k < TOPK - 1:
                        nxt = (b, par, k + 1, zone(b, k + 1))
                    elif not last:
                        nxt = (b + 1, 1 - par, 0, zone(b + 1, 0))
                    else:
                        nxt = None
                    ht(b, k, 0)
                    if nxt:
                        g1(*nxt, 0)
                    ht(b, k, 1)
                    if nxt:
                        g1(*nxt, 1)
                    if e is None:
                        e = zone(b, k)
                    g2(b, par, k, e)
                    e = nxt[3] if nxt else None

            e0 = zone(0, 0)
            g1(0, 0, 0, e0, 0)
            g1(0, 0, 0, e0, 1)
            ffn_body(0, 0, False)
            with pe.Fori(0, (B - 2) // 2) as i:
                ffn_body(i * 2 + 1, 1, False)
                ffn_body(i * 2 + 2, 0, False)
            ffn_body(B - 1, 1, True)


_INS = ["x", "ctx_1024", "mask_Bx1xSxS2_bk1", "g_xattn", "g_ffn", "L0_xattn_Wq", "L0_xattn_bq", "L0_xattn_Wk", "L0_xattn_bk",
        "L0_xattn_Wv", "L0_xattn_bv", "L0_xattn_Wo", "L0_xattn_bo", "L0_ffn_W1", "L0_ffn_b1", "L0_ffn_W2", "L0_ffn_b2",
        "L0_ffn_Wa", "L0_ffn_Wb"]


def kernel(**inputs):
    import numpy as np
    import concourse.bacc as bacc
    from concourse.bass_utils import run_bass_kernel_spmd as run

    nc = bacc.Bacc("TRN2", target_bir_lowering=False, num_devices=1)
    arrays, args = {}, []
    for name in _INS:
        a = np.ascontiguousarray(inputs[name])
        if a.dtype == np.bool_:
            a = a.reshape(B, SQ, SK)
        arrays[f"in_{name}"] = a
        args.append(nc.dram_tensor(f"in_{name}", a.shape, mybir.dt.from_np(a.dtype), kind="ExternalInput").ap())
    args.append(nc.dram_tensor("out_0", (B, SQ, D), F32, kind="ExternalOutput").ap())
    flamingo_layer(nc, *args)
    r = run(nc, [arrays], core_ids=[0])
    return r.results[0]["out_0"]
```

```python
from contextlib import ExitStack

import concourse.bass as bass
from concourse import mybir

F32 = mybir.dt.float32
F16 = mybir.dt.float16
BF16 = mybir.dt.bfloat16
U8 = mybir.dt.uint8
U32 = mybir.dt.uint32
ALU = mybir.AluOpType
ACT = mybir.ActivationFunctionType
AX = mybir.AxisListType

B, SQ, D, SK = 8, 112, 256, 375
NH, HD = 16, 16
DT = D // 128
KC = 3
CK = SK // KC
PAIRS = NH // 2
FF, NZ, RH, TOPK = 1024, 8, 64, 3
FT = FF // 128
EPS = 1e-5
MASKED = -1e15
WSCALE = 64.0
CHUNK = 1024
CHUNKS = 4
NCH = B * CHUNKS
R_USE, V_USE, X_USE, CTX_USE, Q_USE, K_USE, O_USE, X2_USE, FULL_USES = 1, 2, 4, 5, 7, 8, 10, 11, 11
LAST_O_USE, LAST_X2_USE = 4, 5
TAIL_R_USE, TAIL_O_USE, TAIL_X2_USE = 7, 9, 11
ROUTES = ((0, B - 1), (B - 1, 1))
H_USE, L_USE, W_USE = (6, 12), (8, 13), (10, 14)
PREP_USES = 6


class Uses:

    def __init__(self, first, odd, shared):
        self.first, self.odd, self.shared = first, odd, shared

    def n(self, k):
        return self.first + k

    def bank(self, k):
        return self.shared[(self.odd + k) % 2]


class Steps:

    def __init__(self, eng, sem):
        self.eng, self.sem, self.base, self.n = eng, sem, 0, 0

    def begin(self, base):
        self.base, self.n = base, 0

    def done(self, ins):
        ins.then_inc(self.sem, 1)
        self.n += 1

    def link(self, ins):
        self.done(ins)
        self.eng.wait_ge(self.sem, self.base + self.n)


def flamingo_layer(nc, x, ctx, mask, g_xattn, g_ffn, Wq, bq, Wk, bk, Wv, bv, Wo, bo,
                   W1, b1, W2, b2, Wa, Wb, out):
    with ExitStack() as stack:
        def sb(name, shape, dt=F32):
            return stack.enter_context(nc.sbuf_tensor(name, shape, dt))

        def sem(name):
            return stack.enter_context(nc.semaphore(name))

        k_scr = nc.dram_tensor("k_scr", [B, DT, HD, 2, PAIRS, SK], F16).ap()
        q_scr = nc.dram_tensor("q_scr", [B, DT, HD, 4, PAIRS, SQ], F16).ap()
        r_scr = nc.dram_tensor("r_scr", [B, SQ, D], F32).ap()
        x2_scr = nc.dram_tensor("x2_scr", [B, 128, 2 * DT * SQ], F16).ap()

        wa = sb("wa", [128, NZ * 2 * DT * FF], F16)
        wb = sb("wb", [128, NZ * 2 * FT * D], F16)
        stage = sb("stage", [128, 2, CHUNK])
        wqkvo = sb("wqkvo", [128, 4, DT, D])
        bq_c = sb("bq_c", [128, DT])
        bk_c = sb("bk_c", [128, DT])
        bv_r = sb("bv_r", [128, D])
        bo_r = sb("bo_r", [128, D])
        w1_s = sb("w1_s", [128, DT, RH])
        w2_s = sb("w2_s", [RH, NZ])
        b1_c = sb("b1_c", [RH, 1])
        b2_r = sb("b2_r", [B, NZ])
        gates = sb("gates", [128, 2])
        tgate = sb("tgate", [128, 2])
        tf_w = sb("tf_w", [128, 1])
        ident = sb("ident", [128, 128])
        ident_b = sb("ident_b", [SQ, SQ], BF16)
        half = sb("half", [128, 1])
        ones = sb("ones", [B, 128])
        ctx_s = sb("ctx_s", [CK, KC, D])
        ctxT = sb("ctxT", [128, DT, SK])
        k_hl = sb("k_hl", [128, DT, 2, SK], F16)
        q_f = sb("q_f", [128, DT, SQ])
        q_hl = sb("q_hl", [128, DT, 2, 2, SQ], F16)
        kst = sb("kst", [128, 2, PAIRS * SK], F16)
        qst = sb("qst", [128, 2, PAIRS, SQ], F16)
        vpad = sb("vpad", [CK, KC, PAIRS, 64])
        probs = sb("probs", [SQ, 2, 2, SK])
        pT = sb("pT", [CK, 2, KC, 2 * SQ])
        mask_s = sb("mask_s", [SQ, SK], U8)
        maskb = sb("maskb", [SQ, 2, SK], BF16)
        xa = sb("xa", [SQ, D])
        xT = sb("xT", [128, DT * SQ])
        xr = sb("xr", [SQ, D])
        yo = sb("yo", [SQ, D])
        x2 = sb("x2", [SQ, D])
        res = sb("res", [SQ, D])
        x2T = sb("x2T", [128, 2, DT * SQ], F16)
        stat = sb("stat", [SQ, 6])
        mv = sb("mv", [SQ, 2])
        ve = sb("ve", [SQ, 1])
        rstd = sb("rstd", [SQ, 1])
        stat2 = sb("stat2", [SQ, 6])
        mv2 = sb("mv2", [SQ, 2])
        ve2 = sb("ve2", [SQ, 1])
        rstd2 = sb("rstd2", [SQ, 1])
        negmax = sb("negmax", [SQ, NH])
        rowsum = sb("rowsum", [SQ, 2, NH])
        rinv = sb("rinv", [SQ, NH])
        rexp = sb("rexp", [SQ, NH, HD])
        rT = sb("rT", [128, DT * SQ])
        oT = sb("oT", [128, DT * SQ])
        o_raw = sb("o_raw", [128, DT * SQ])
        pooled = sb("pooled", [128, DT, B])
        h_s = sb("h_s", [RH, B])
        lg = sb("lg", [B, NZ])
        top = sb("top", [B, NZ])
        nmx = sb("nmx", [B, 1])
        ez = sb("ez", [B, NZ])
        zs = sb("zs", [B, 1])
        zr = sb("zr", [B, 1])
        pz = sb("pz", [B, NZ])
        ptop = sb("ptop", [B, NZ])
        pidx = [sb("pidx0", [B, NZ], U32), sb("pidx1", [1, NZ], U32)]
        ts = sb("ts", [B, 1])
        tr = sb("tr", [B, 1])
        wz = sb("wz", [B, TOPK])
        wdiag = sb("wdiag", [B, B, TOPK])
        wbc = sb("wbc", [128, B * TOPK])
        wcur = sb("wcur", [128, 2, TOPK])
        idx_row = sb("idx_row", [1, B * NZ], U32)
        x2b = ctxT[:].rearrange("p a f -> p (a f)")[:, 0:2 * DT * SQ].bitcast(F16).rearrange("p (a f) -> p a f", a=2)
        h_f = kst[:].rearrange("p a f -> p (a f)")[0:SQ, 0:2 * 2 * FF].bitcast(F32)
        hT = stage[:].rearrange("p a f -> p (a f)")[:, 0:2 * FT * SQ].bitcast(F16)
        rb = [xa[:], xr[:]]
        ob = [yo[:], x2[:]]

        bank = stack.enter_context(nc.psum_tensor("bank", [128, 8, 512], F32))
        flat = bank[:].rearrange("p a f -> p (a f)")
        PTB = 4 * 512
        OB = 256
        shared = [bank[:, 6, :], bank[:, 7, :]]

        def uses(b, par):
            if isinstance(b, int) and b == 0:
                return Uses(PREP_USES - 1, (PREP_USES - 1) % 2, shared)
            before_1 = PREP_USES - 1 + X2_USE - 2
            return Uses(before_1 + (b - 1) * FULL_USES, (before_1 + 1 + par) % 2, shared)

        names = ("wk_loaded wq_loaded wv_loaded wo_loaded bk_loaded bq_loaded bv_loaded const_loaded g_loaded ident_ready setup_pool setup_dve setup_act x_loaded ctx_loaded mask_loaded xr_loaded "
                 "k_written0 k_written1 q_written k_stacked0 k_stacked1 k_stacked2 q_stacked res_written x2_written "
                 "chunk_loaded0 chunk_loaded1 scaled hi_done lo_done "
                 "pe_s dve_max act_exp pe_t act_pt pe_pv act_o dve_o misc_full misc_free "
                 "khi_done klo_done qf_done qhi_done qlo_done mask_ready ln1_var ln1_rstd xn_done xa_used ctx_used "
                 "vpad_ready rexp_done ln2_var ln2_rstd x2_done x2hi_done x2lo_done res_done xr_used pool_chain "
                 "h_act nmx_done wdiag_done e_done idx_done idx_loaded route_done wcur_done "
                 "dve_passed pool_passed dve_step g1_done gelu_done ht_full hthi_done htlo_done g2_done y_done r_loaded x2b_loaded out_written").split()
        s = {n: sem(n) for n in names}
        k_written = [s["k_written0"], s["k_written1"]]
        chunk_loaded = [s["chunk_loaded0"], s["chunk_loaded1"]]

        def view_w(ap):
            return ap.rearrange("(t p) n -> p t n", p=128)

        block = stack.enter_context(nc.Block())

        def chunk_dst(z, c, hl):
            t = wa if c < 2 else wb
            return t[:, bass.ds(z * (4 * CHUNK) + hl * (2 * CHUNK) + (c % 2) * CHUNK, CHUNK)]

        def alone(eng, sem_, n, passed):
            eng.wait_ge(sem_, n)
            eng.sem_inc(passed, 1)

        def over_batches(eng, body):
            body(0, 0)
            with eng.Fori(0, (B - 2) // 2) as i:
                body(i * 2 + 1, 1)
                body(i * 2 + 2, 0)
            body(B - 1, 1)

        @block.sync
        def _(sp):
            for n in ("xr_used", "x2_written", "res_written", "y_done", "out_written"):
                sp.sem_inc(s[n], 1)
            def load_prep(b):
                sp.dma_start(xa[:, :], x[bass.ds(b, 1), :, :].rearrange("o s d -> (o s) d")).then_inc(s["x_loaded"], 16)
                sp.dma_start(ctx_s[:, :, :], ctx[bass.ds(b, 1), :, :].rearrange("o (c r) d -> r (o c) d", r=CK)).then_inc(s["ctx_loaded"], 16)
                sp.dma_start(mask_s[:, :], mask[bass.ds(b, 1), :, :].rearrange("o s d -> (o s) d")).then_inc(s["mask_loaded"], 16)

            def stack_q(b):
                sp.wait_ge(s["qlo_done"], b + 1)
                for t in range(DT):
                    sp.dma_start(q_scr[bass.ds(b, 1), t, :, :, :, :].rearrange("o i a j f -> j (o i) a f"),
                                 q_hl[:, t, :, :, :].rearrange("p r a f -> p (r a) f")).then_inc(s["q_written"], 16)

            def stack_k(b, t):
                sp.wait_ge(s["klo_done"], b * 2 + t + 1)
                sp.dma_start(k_scr[bass.ds(b, 1), t, :, :, :, :].rearrange("o i a j f -> j (o i) a f"),
                             k_hl[:, t, :, :]).then_inc(k_written[t], 16)

            def read_q(b, par):
                sp.wait_ge(s["q_written"], b * 32 + 32)
                run = PAIRS * SQ
                sp.dma_start(qst[:, par, :, :].rearrange("p a f -> p (a f)"),
                             bass.AP(q_scr.tensor, b * (DT * HD * 4 * run), [[run, 128], [1, run]])).then_inc(s["q_stacked"], 16)

            def read_k(b, par, t, lo, hi, stacked):
                sp.wait_ge(k_written[t], b * 16 + 16)
                sp.dma_start(kst[64 * t:64 * t + 64, par, lo * SK:hi * SK],
                             bass.AP(k_scr.tensor, (b * DT + t) * (HD * 2 * PAIRS * SK) + lo * SK,
                                     [[PAIRS * SK, HD * 2], [0, 2], [1, (hi - lo) * SK]])).then_inc(stacked, 16)

            def stack_all(b, par):
                stack_q(b)
                stack_k(b, 0)
                stack_k(b, 1)
                read_q(b, par)
                read_k(b, par, 0, 0, PAIRS, s["k_stacked0"])
                read_k(b, par, 1, 0, PAIRS // 2, s["k_stacked1"])
                read_k(b, par, 1, PAIRS // 2, PAIRS, s["k_stacked2"])

            load_prep(0)
            sp.dma_start(wqkvo[:, 2, :, :], view_w(Wv)).then_inc(s["wv_loaded"], 16)
            stack_all(0, 0)
            sp.wait_ge(s["xa_used"], 1)
            sp.wait_ge(s["ctx_used"], 1)
            sp.wait_ge(s["mask_ready"], 1)
            load_prep(1)
            for t in range(DT):
                for j in range(4):
                    sp.dma_start(wqkvo[32 * j:32 * j + 32, 3, t, :], bass.AP(Wo.tensor, (4 * t + j) * HD * D,
                                 [[PAIRS * HD * D, 2], [D, HD], [1, D]])).then_inc(s["wo_loaded"], 16)

            def body(b, par):
                first = isinstance(b, int) and b == 0
                last = isinstance(b, int) and b == B - 1
                if not first:
                    sp.wait_ge(s["xr_used"], b)
                    sp.dma_start(xr[:, :], x[bass.ds(b - 1, 1), :, :].rearrange("o s d -> (o s) d")).then_inc(s["xr_loaded"], 16)
                if not last:
                    stack_all(b + 1, 1 - par)
                if not last:
                    sp.wait_ge(s["xa_used"], b + 2)
                    sp.wait_ge(s["ctx_used"], b + 2)
                    sp.wait_ge(s["mask_ready"], b + 2)
                    if isinstance(b, int):
                        if b + 2 < B:
                            load_prep(b + 2)
                    else:
                        load_prep(b + 2)
                if not first:
                    store_post(b - 1)

            def store_post(b):
                sp.wait_ge(s["res_done"], b + 1)
                sp.dma_start(r_scr[bass.ds(b, 1), :, :].rearrange("o s d -> (o s) d"), res[:, :]).then_inc(s["res_written"], 16)
                sp.wait_ge(s["x2lo_done"], b + 1)
                sp.dma_start(x2_scr[bass.ds(b, 1), :, :].rearrange("o p f -> (o p) f"),
                             x2T[:].rearrange("p a f -> p (a f)")).then_inc(s["x2_written"], 16)

            body(0, 0)
            with sp.Fori(0, (B - 4) // 2) as i:
                body(i * 2 + 1, 1)
                body(i * 2 + 2, 0)
            for b in range(B - 3, B):
                body(b, b % 2)
            sp.wait_ge(s["xr_used"], B)
            sp.dma_start(xr[:, :], x[B - 1, :, :]).then_inc(s["xr_loaded"], 16)

            def load_r(b, par):
                sp.dma_start(rb[par], r_scr[bass.ds(b, 1), :, :].rearrange("o s d -> (o s) d")).then_inc(s["r_loaded"], 16)

            def load_x2(b, par):
                sp.dma_start(x2b[:, par, :], x2_scr[bass.ds(b, 1), :, :].rearrange("o p f -> (o p) f")).then_inc(s["x2b_loaded"], 16)

            def store_index(g):
                sp.wait_ge(s["idx_done"], g + 1)
                b0, n = ROUTES[g]
                sp.dma_start(idx_row[:, b0 * NZ:(b0 + n) * NZ], pidx[g][0:n, :]).then_inc(s["idx_loaded"], 16)

            def store_out(b, par):
                sp.wait_ge(s["y_done"], b + 2)
                sp.dma_start(out[bass.ds(b, 1), :, :].rearrange("o s d -> (o s) d"), ob[par]).then_inc(s["out_written"], 16)

            sp.wait_ge(s["res_written"], 16 * (B - 1) + 1)
            sp.wait_ge(s["x2_written"], 16 * (B - 1) + 1)
            sp.wait_ge(s["xa_used"], B)
            sp.wait_ge(s["vpad_ready"], B)
            load_r(0, 0)
            load_x2(0, 0)
            store_index(0)
            sp.wait_ge(s["x2b_loaded"], 16)
            load_x2(1, 1)
            store_post(B - 1)
            sp.wait_ge(s["xr_used"], B + 1)
            sp.wait_ge(s["r_loaded"], 16)
            load_r(1, 1)
            store_index(1)
            sp.wait_ge(s["res_written"], 16 * B + 1)
            sp.wait_ge(s["x2_written"], 16 * B + 1)
            with sp.Fori(0, (B - 2) // 2) as i:
                for par in range(2):
                    b = i * 2 + par
                    store_out(b, par)
                    sp.wait_ge(s["r_loaded"], b * 16 + 32)
                    sp.wait_ge(s["x2b_loaded"], b * 16 + 32)
                    load_r(b + 2, par)
                    load_x2(b + 2, par)
            store_out(B - 2, 0)
            store_out(B - 1, 1)
            sp.wait_ge(s["out_written"], 16 * B + 1)

        @block.gpsimd
        def _(pool):
            g = nc.gpsimd
            chain = Steps(pool, s["pool_chain"])
            def load_chunk(b, c):
                if c < 2:
                    src = Wa[bass.ds(b, 1), c * 128:(c + 1) * 128, :].rearrange("o p f -> (o p) f")
                    dst = stage[:, c % 2, :]
                else:
                    src = Wb[bass.ds(b, 1), (c - 2) * 512:(c - 1) * 512, :].rearrange("o (f p) n -> p (o f) n", p=128)
                    dst = stage[:, c % 2, :].rearrange("p (f n) -> p f n", n=D)
                g.dma_start(dst, src).then_inc(chunk_loaded[c % 2], 16)

            chain.link(g.memset(ident[:, :], 0.0))
            chain.link(g.affine_select(out=ident[:, :], in_=ident[:, :], compare_op=ALU.not_equal, fill=1.0,
                                       base=0, pattern=[[-1, 128]], channel_multiplier=1))
            pool.sem_inc(s["ident_ready"], 1)
            chain.link(g.tensor_copy(ident_b[:, :], ident[0:SQ, 0:SQ]))
            chain.link(g.memset(half[:, :], -0.5))
            chain.link(g.memset(ones[:, :], 1.0))
            def pow_rstd(dst, src, ready, n, signal):
                pool.wait_ge(ready, n)
                g.tensor_tensor(dst, src, half[0:SQ, :], ALU.pow).then_inc(signal, 1)

            load_chunk(0, 0)
            load_chunk(0, 1)
            pow_rstd(rstd[:, :], ve[:, :], s["ln1_var"], 1, s["ln1_rstd"])
            g.memset(vpad[:].rearrange("p a b c -> p (a b c)"), 0.0).then_inc(s["setup_pool"], 1)
            g.dma_start(bv_r[:, :], bass.AP(bv.tensor, 0, [[0, 128], [1, D]])).then_inc(s["bv_loaded"], 16)

            def small_loads():
                g.dma_start(bo_r[:, :], bass.AP(bo.tensor, 0, [[0, 128], [1, D]])).then_inc(s["const_loaded"], 16)
                g.dma_start(w1_s[:, :, :], W1.rearrange("(t p) n -> p t n", p=128)).then_inc(s["const_loaded"], 16)
                g.dma_start(w2_s[:, :], W2).then_inc(s["const_loaded"], 16)
                g.dma_start(b1_c[:, :], b1.rearrange("(p o) -> p o", o=1), allow_slow_non_contiguous=True).then_inc(s["const_loaded"], 16)
                g.dma_start(b2_r[:, :], bass.AP(b2.tensor, 0, [[0, B], [1, NZ]])).then_inc(s["const_loaded"], 16)

            def scale_chunk(b, c):
                st = stage[:, c % 2, :]
                alone(pool, chunk_loaded[c % 2], b * 32 + 16 * (c // 2) + 16, s["pool_passed"])
                g.tensor_scalar(st, st, WSCALE, 1.0, ALU.mult, ALU.mult).then_inc(s["scaled"], 1)

            def lo_chunk(b, c):
                alone(pool, s["hi_done"], b * CHUNKS + c + 1, s["pool_passed"])
                g.tensor_tensor(chunk_dst(b, c, 1), stage[:, c % 2, :], chunk_dst(b, c, 0), ALU.subtract).then_inc(s["lo_done"], 1)

            def reload(b, c):
                alone(pool, s["lo_done"], b * CHUNKS + c - 1, s["pool_passed"])
                load_chunk(b, c)

            def body(b, par):
                first = isinstance(b, int) and b == 0
                last = isinstance(b, int) and b == B - 1
                if not last:
                    pow_rstd(rstd[:, :], ve[:, :], s["ln1_var"], b + 2, s["ln1_rstd"])
                if not first:
                    for c in range(2):
                        lo_chunk(b, c)
                        reload(b, c + 2)
                scale_chunk(b, 2)
                scale_chunk(b, 3)
                lo_chunk(b, 2)
                if not last:
                    reload(b + 1, 0)
                if not first:
                    pow_rstd(rstd2[:, :], ve2[:, :], s["ln2_var"], b, s["ln2_rstd"])
                lo_chunk(b, 3)
                if not last:
                    reload(b + 1, 1)
                    scale_chunk(b + 1, 0)
                    scale_chunk(b + 1, 1)

            scale_chunk(0, 0)
            scale_chunk(0, 1)
            small_loads()
            for c in range(2):
                lo_chunk(0, c)
                reload(0, c + 2)
            over_batches(pool, body)
            pow_rstd(rstd2[:, :], ve2[:, :], s["ln2_var"], B, s["ln2_rstd"])

        @block.scalar
        def _(act):
            a = nc.scalar
            for n, w, name in ((0, Wq, "wq_loaded"), (1, Wk, "wk_loaded")):
                a.dma_start(wqkvo[:, n, :, :], view_w(w)).then_inc(s[name], 16)
            a.dma_start(bk_c[:, :], bk.rearrange("(t p) -> p t", p=128), allow_slow_non_contiguous=True).then_inc(s["bk_loaded"], 16)
            a.dma_start(bq_c[:, :], bq.rearrange("(t p) -> p t", p=128), allow_slow_non_contiguous=True).then_inc(s["bq_loaded"], 16)
            a.dma_start(gates[:, 0:1], bass.AP(g_xattn.tensor, 0, [[0, 128], [1, 1]])).then_inc(s["g_loaded"], 16)
            a.dma_start(gates[:, 1:2], bass.AP(g_ffn.tensor, 0, [[0, 128], [1, 1]])).then_inc(s["g_loaded"], 16)
            act.wait_ge(s["g_loaded"], 32)
            a.activation(tgate[:, :], gates[:, :], ACT.Tanh).then_inc(s["setup_act"], 1)

            def exp_head(b, par, p, e):
                act.wait_ge(s["dve_max"], b * NH + 2 * p + e + 1)
                if e == 0:
                    if not (isinstance(b, int) and b == 0 and p < 2):
                        act.wait_ge(s["pe_t"], b * PAIRS + p - 1)
                h = 2 * p + e
                a.activation(probs[:, p % 2, e, :], bank[0:SQ, 2 * (p % 2) + e, 0:SK], ACT.Exp,
                             bias=negmax[:, h:h + 1], accum_out=rowsum[:, par, h:h + 1]).then_inc(s["act_exp"], 1)

            def pt_copy(b, p):
                act.wait_ge(s["pe_t"], b * PAIRS + p + 1)
                if not (isinstance(b, int) and b == 0 and p < 2):
                    act.wait_ge(s["pe_pv"], b * PAIRS + p - 1)
                a.activation(pT[:, p % 2, :, :], flat[0:CK, PTB:PTB + KC * 256].rearrange("p (c f) -> p c f", c=KC)[:, :, 0:2 * SQ],
                             ACT.Copy).then_inc(s["act_pt"], 1)

            def o_copy(b):
                act.wait_ge(s["pe_pv"], b * PAIRS + PAIRS)
                if not (isinstance(b, int) and b == 0):
                    act.wait_ge(s["dve_o"], b)
                a.activation(o_raw[:, :], flat[:, PTB + 512 + OB:PTB + 512 + OB + DT * SQ], ACT.Copy).then_inc(s["act_o"], 1)

            def k_hi(b, t, u, k):
                act.wait_ge(s["misc_full"], u.n(k))
                if not (isinstance(b, int) and b == 0):
                    act.wait_ge(k_written[t], b * 16)
                a.activation(k_hl[:, t, 0, :], u.bank(k)[:, 0:SK], ACT.Identity, bias=bk_c[:, t:t + 1]).then_inc(s["khi_done"], 1)

            def q_hi(b):
                act.wait_ge(s["qf_done"], b + 1)
                if not (isinstance(b, int) and b == 0):
                    act.wait_ge(s["q_written"], b * 32)
                a.activation(q_hl[:, :, :, 0, :], bass.AP(q_f, 0, [[DT * SQ, 128], [SQ, DT], [0, 2], [1, SQ]]), ACT.Copy).then_inc(s["qhi_done"], 1)

            def x2_hi(b, u, k):
                act.wait_ge(s["misc_full"], u.n(k))
                if not (isinstance(b, int) and b == 0):
                    act.wait_ge(s["x2_written"], b * 16 + 1)
                a.activation(x2T[:, 0, :], u.bank(k)[:, 0:DT * SQ], ACT.Copy).then_inc(s["x2hi_done"], 1)

            prep_u = Uses(0, 0, shared)
            act.wait_ge(s["bk_loaded"], 16)
            q_hi(0)
            k_hi(0, 0, prep_u, 5)
            k_hi(0, 1, prep_u, 6)
            exp_head(0, 0, 0, 0)
            exp_head(0, 0, 0, 1)
            exp_head(0, 0, 1, 0)

            def body(b, par):
                first = isinstance(b, int) and b == 0
                last = isinstance(b, int) and b == B - 1
                u = uses(b, par)

                def exps(p, e):
                    if p < PAIRS:
                        exp_head(b, par, p, e)
                    elif not last:
                        exp_head(b + 1, 1 - par, p - PAIRS, e)

                for p in range(PAIRS):
                    pt_copy(b, p)
                    if p == 0 and not first:
                        o_copy(b - 1)
                    exps(p + 1, 1)
                    if p == 2 and not last:
                        k_hi(b + 1, 0, u, K_USE)
                        k_hi(b + 1, 1, u, K_USE + 1)
                    if p == 6 and not first:
                        x2_hi(b - 1, u, X2_USE if not last else LAST_X2_USE)
                    exps(p + 2, 0)
                    if p == 1 and not last:
                        q_hi(b + 1)

            over_batches(act, body)
            u = uses(B - 1, 1)

            def route_hidden(g):
                b0, n = ROUTES[g]
                act.wait_ge(s["misc_full"], u.n(H_USE[g]))
                a.activation(h_s[:, 0:n], u.bank(H_USE[g])[0:RH, 0:n], ACT.Tanh, bias=b1_c[:, :], scale=1.0 / SQ).then_inc(s["h_act"], 1)

            def route_exp(g):
                b0, n = ROUTES[g]
                act.wait_ge(s["nmx_done"], g + 1)
                a.activation(ez[0:n, :], lg[0:n, :], ACT.Exp, bias=nmx[0:n, :], accum_out=zs[0:n, :]).then_inc(s["e_done"], 1)

            act.wait_ge(s["const_loaded"], 80)
            route_hidden(0)
            o_copy(B - 1)
            route_exp(0)
            act.wait_ge(s["lo_done"], NCH)

            def gelu(u_done, hf):
                act.wait_ge(s["g1_done"], u_done * 2 + hf + 1)
                act.wait_ge(s["ht_full"], u_done * 2)
                a.activation(h_f[:, hf * 512:(hf + 1) * 512], bank[0:SQ, hf, :], ACT.Gelu_apprx_tanh,
                             scale=1.0 / WSCALE).then_inc(s["gelu_done"], 1)

            def ht_hi(b, par, k, hf):
                u = b * TOPK + k
                if k == 0 and hf == 0:
                    act.wait_ge(s["wcur_done"], b + 1)
                act.wait_ge(s["ht_full"], u * 2 + hf + 1)
                if not (isinstance(u, int) and u == 0):
                    act.wait_ge(s["g2_done"], u)
                a.activation(hT[:, hf * 448:hf * 448 + 448], bank[:, 2 + hf, 0:448], ACT.Copy,
                             scale=wcur[:, par, k:k + 1]).then_inc(s["hthi_done"], 1)

            def ffn_body(b, par, last):
                for k in range(TOPK):
                    n = b * TOPK + k
                    if isinstance(b, int) and b == 0 and k == 1:
                        route_hidden(1)
                    for hf in range(2):
                        ht_hi(b, par, k, hf)
                        if not (last and k == TOPK - 1):
                            gelu(n + 1, hf)
                    if isinstance(b, int) and b == 0:
                        if k == 0:
                            x2_hi(B - 1, u, TAIL_X2_USE)
                        if k == 1:
                            route_exp(1)

            gelu(0, 0)
            gelu(0, 1)
            ffn_body(0, 0, False)
            with act.Fori(0, (B - 2) // 2) as i:
                ffn_body(i * 2 + 1, 1, False)
                ffn_body(i * 2 + 2, 0, False)
            ffn_body(B - 1, 1, True)


        @block.vector
        def _(dve):
            v = nc.vector
            st = Steps(dve, s["dve_step"])
            def mask_bias(b, par):
                dve.wait_ge(s["mask_loaded"], b * 16 + 16)
                if not (isinstance(b, int) and b < 2):
                    dve.wait_ge(s["pe_s"], b * NH - NH)
                v.tensor_scalar(maskb[:, par, :], mask_s[:, :], MASKED, 1.0, ALU.mult, ALU.mult).then_inc(s["mask_ready"], 1)

            def row_max(b, p):
                for e in range(2):
                    h = 2 * p + e
                    dve.wait_ge(s["pe_s"], b * NH + h + 1)
                    v.tensor_reduce(negmax[:, h:h + 1], bank[0:SQ, 2 * (p % 2) + e, 0:SK], AX.X, ALU.max,
                                    negate=True).then_inc(s["dve_max"], 1)

            def full(u, k):
                dve.wait_ge(s["misc_full"], u.n(k))

            def layernorm_stats(src, stat_, mv_, ve_, ready):
                st.link(v.bn_stats(stat_[:, :], src))
                dve.sem_inc(s["dve_passed"], 1)
                st.link(v.bn_aggr(mv_[:, :], stat_[:, :]))
                v.tensor_scalar(ve_[:, :], mv_[:, 1:2], EPS, None, ALU.add).then_inc(ready, 1)

            def ln1_stats(b):
                dve.wait_ge(s["x_loaded"], b * 16 + 16)
                layernorm_stats(xa[:, :], stat, mv, ve, s["ln1_var"])

            def ln1_apply(b):
                dve.wait_ge(s["ln1_rstd"], b + 1)
                v.tensor_scalar(xa[:, :], xa[:, :], mv[:, 0:1], rstd[:, :], ALU.subtract, ALU.mult).then_inc(s["xn_done"], 1)

            def ctx_copy(t, u, k):
                full(u, k)
                if t == DT - 1:
                    dve.sem_inc(s["ctx_used"], 1)
                v.tensor_copy(ctxT[:, t, :], u.bank(k)[:, 0:SK]).then_inc(s["misc_free"], 1)

            def x_copy(u, k):
                full(u, k)
                dve.sem_inc(s["xa_used"], 1)
                v.tensor_copy(xT[:, :], u.bank(k)[:, 0:DT * SQ]).then_inc(s["misc_free"], 1)

            def k_lo(b, t, u, k):
                dve.wait_ge(s["khi_done"], b * 2 + t + 1)
                v.scalar_tensor_tensor(out=k_hl[:, t, 1, :], in0=u.bank(k)[:, 0:SK], scalar=bk_c[:, t:t + 1],
                                       in1=k_hl[:, t, 0, :], op0=ALU.add, op1=ALU.subtract).then_inc(s["klo_done"], 1)
                dve.wait_ge(s["klo_done"], b * 2 + t + 1)
                dve.sem_inc(s["misc_free"], 1)

            def q_full(b, u, k):
                full(u, k)
                if not (isinstance(b, int) and b == 0):
                    dve.wait_ge(s["q_written"], b * 32)
                for t in range(DT):
                    ins = v.tensor_scalar(q_f[:, t, :], u.bank(k)[:, t * SQ:(t + 1) * SQ], bq_c[:, t:t + 1], HD ** -0.5,
                                          ALU.add, ALU.mult)
                    if t == 0:
                        st.done(ins)
                ins.then_inc(s["qf_done"], 1)
                dve.wait_ge(s["qf_done"], b + 1)
                dve.sem_inc(s["misc_free"], 1)

            def q_lo(b):
                dve.wait_ge(s["qhi_done"], b + 1)
                v.tensor_tensor(q_hl[:, :, :, 1, :], bass.AP(q_f, 0, [[DT * SQ, 128], [SQ, DT], [0, 2], [1, SQ]]),
                                q_hl[:, :, :, 0, :], ALU.subtract).then_inc(s["qlo_done"], 1)

            def v_copy(c, src):
                out_ = bass.AP(vpad, c * PAIRS * 64, [[KC * PAIRS * 64, CK], [64, PAIRS], [48, 2], [1, HD]])
                return v.tensor_tensor(out_, src.rearrange("p (e q i) -> p q e i", e=2, i=HD),
                                       bv_r[0:CK, :].rearrange("p (e q i) -> p q e i", e=2, i=HD), ALU.add)

            def v_stage(b, u):
                if not (isinstance(b, int) and b == 0):
                    dve.wait_ge(s["pe_pv"], b * PAIRS)
                full(u, V_USE)
                st.done(v_copy(0, u.bank(V_USE)[0:CK, 0:D]))
                v_copy(1, u.bank(V_USE)[0:CK, D:2 * D]).then_inc(s["misc_free"], 1)
                full(u, V_USE + 1)
                v_copy(2, u.bank(V_USE + 1)[0:CK, 0:D]).then_inc(s["misc_free"], 1)
                dve.wait_ge(s["dve_step"], st.base + st.n)
                dve.wait_ge(s["misc_free"], u.n(V_USE + 1))
                dve.sem_inc(s["vpad_ready"], 1)

            def row_sums(b, par):
                dve.wait_ge(s["act_exp"], b * NH + NH)
                st.link(v.reciprocal(rinv[:, :], rowsum[:, par, :]))
                v.tensor_copy(rexp[:, :, :], bass.AP(rinv, 0, [[NH, SQ], [1, NH], [0, HD]])).then_inc(s["rexp_done"], 1)

            def rt_copy(u, k):
                full(u, k)
                v.tensor_copy(rT[:, :], u.bank(k)[:, 0:DT * SQ]).then_inc(s["misc_free"], 1)
                dve.wait_ge(s["misc_free"], u.n(k))

            def o_scale(b):
                dve.wait_ge(s["act_o"], b + 1)
                v.tensor_tensor(oT[:, :], o_raw[:, :], rT[:, :], ALU.mult).then_inc(s["dve_o"], 1)

            def residual(b, u, k):
                full(u, k)
                v.tensor_tensor(yo[:, :], u.bank(k)[0:SQ, 0:D], bo_r[0:SQ, :], ALU.add).then_inc(s["misc_free"], 1)
                dve.wait_ge(s["misc_free"], u.n(k))
                dve.wait_ge(s["xr_loaded"], b * 16 + 16)
                st.link(v.scalar_tensor_tensor(out=xr[:, :], in0=yo[:, :], scalar=tgate[0:SQ, 0:1], in1=xr[:, :], op0=ALU.mult, op1=ALU.add))
                layernorm_stats(xr[:, :], stat2, mv2, ve2, s["ln2_var"])

            def ln2_apply(b):
                dve.wait_ge(s["ln2_rstd"], b + 1)
                v.tensor_scalar(x2[:, :], xr[:, :], mv2[:, 0:1], rstd2[:, :], ALU.subtract, ALU.mult).then_inc(s["x2_done"], 1)
                dve.wait_ge(s["x2_done"], b + 1)
                if not (isinstance(b, int) and b == 0):
                    dve.wait_ge(s["res_written"], b * 16 + 1)
                v.scalar_tensor_tensor(out=res[:, :], in0=x2[:, :], scalar=tgate[0:SQ, 1:2], in1=xr[:, :], op0=ALU.mult,
                                       op1=ALU.add).then_inc(s["res_done"], 1)
                dve.wait_ge(s["res_done"], b + 1)
                dve.sem_inc(s["xr_used"], 1)

            def x2_lo(b, u, k):
                dve.wait_ge(s["x2hi_done"], b + 1)
                src = u.bank(k)[:, 0:DT * SQ]
                v.tensor_tensor(x2T[:, 1, :], src, x2T[:, 0, :], ALU.subtract).then_inc(s["x2lo_done"], 1)
                dve.wait_ge(s["x2lo_done"], b + 1)
                v.tensor_reduce(pooled[:, :, bass.ds(b, 1)], src.rearrange("p (t f) -> p t f", t=DT), AX.X,
                                ALU.add).then_inc(s["misc_free"], 1)

            def w_hi(b, c):
                alone(dve, s["scaled"], b * CHUNKS + c + 1, s["dve_passed"])
                v.tensor_copy(chunk_dst(b, c, 0), stage[:, c % 2, :]).then_inc(s["hi_done"], 1)

            prep_u = Uses(0, 0, shared)
            ln1_stats(0)
            ln1_apply(0)
            x_copy(prep_u, 1)
            ctx_copy(0, prep_u, 2)
            ctx_copy(1, prep_u, 3)
            dve.wait_ge(s["bq_loaded"], 16)
            q_full(0, prep_u, 4)
            q_lo(0)
            dve.wait_ge(s["bk_loaded"], 16)
            k_lo(0, 0, prep_u, 5)
            k_lo(0, 1, prep_u, 6)
            mask_bias(0, 0)
            dve.wait_ge(s["setup_act"], 1)
            v.tensor_scalar(tf_w[:, :], tgate[:, 1:2], 1.0 / WSCALE, None, ALU.mult).then_inc(s["setup_dve"], 1)
            dve.wait_ge(s["bv_loaded"], 16)
            dve.wait_ge(s["setup_pool"], 1)
            v_stage(0, uses(0, 0))
            w_hi(0, 0)
            w_hi(0, 1)
            row_max(0, 0)
            row_max(0, 1)
            SET = st.n
            counts = {}


            def body(b, par):
                first = isinstance(b, int) and b == 0
                last = isinstance(b, int) and b == B - 1
                st.begin(SET if first else SET + FIRST + FULL * (b - 1))
                u = uses(b, par)
                for p in range(PAIRS):
                    if p == 0:
                        if not first:
                            rt_copy(u, R_USE)
                        if not last:
                            ln1_stats(b + 1)
                        if not first:
                            o_scale(b - 1)
                            v_stage(b, u)
                    if p == 1 and not last:
                        x_copy(u, X_USE)
                        ctx_copy(0, u, CTX_USE)
                    if p == 2 and not last:
                        q_lo(b + 1)
                        k_lo(b + 1, 0, u, K_USE)
                    if p < PAIRS - 2:
                        row_max(b, p + 2)
                    elif not last:
                        row_max(b + 1, p - PAIRS + 2)
                    if p == 0:
                        if not last:
                            ln1_apply(b + 1)
                        if not first:
                            w_hi(b, 1)
                    if p == 1 and not last:
                        ctx_copy(1, u, CTX_USE + 1)
                        q_full(b + 1, u, Q_USE)
                    if p == 2 and not last:
                        k_lo(b + 1, 1, u, K_USE + 1)
                    if p == 3:
                        if not last:
                            mask_bias(b + 1, 1 - par)
                        w_hi(b, 2)
                    if p == 3 and not first:
                        residual(b - 1, u, LAST_O_USE if last else O_USE)
                    if p == 5 and not first:
                        ln2_apply(b - 1)
                    if p == 6:
                        row_sums(b, par)
                        if not first:
                            x2_lo(b - 1, u, LAST_X2_USE if last else X2_USE)
                    if p == 4:
                        w_hi(b, 3)
                    if p == 7 and not last:
                        w_hi(b + 1, 0)
                if first:
                    dve.wait_ge(s["const_loaded"], 80)
                counts["last" if last else "first" if first else "full"] = st.n

            FIRST, FULL = 4, 8
            over_batches(dve, body)
            assert counts["first"] == FIRST and counts["full"] == FULL, counts
            st.begin(SET + FIRST + FULL * (B - 2) + counts["last"])
            u = uses(B - 1, 1)

            def route_logits(g):
                b0, n = ROUTES[g]
                full(u, L_USE[g])
                st.link(v.tensor_tensor(lg[0:n, :], u.bank(L_USE[g])[0:n, 0:NZ], b2_r[0:n, :], ALU.add))
                dve.sem_inc(s["misc_free"], 1)
                st.link(v.max(top[0:n, :], lg[0:n, :]))
                v.tensor_scalar(nmx[0:n, :], top[0:n, 0:1], -1.0, None, ALU.mult).then_inc(s["nmx_done"], 1)

            def route_top(g):
                b0, n = ROUTES[g]
                dve.wait_ge(s["e_done"], g + 1)
                st.link(v.reciprocal(zr[0:n, :], zs[0:n, :]))
                st.link(v.tensor_scalar(pz[0:n, :], ez[0:n, :], zr[0:n, :], None, ALU.mult))
                st.link(v.max(ptop[0:n, :], pz[0:n, :]))
                v.max_index(pidx[g][0:n, :], ptop[0:n, :], pz[0:n, :]).then_inc(s["idx_done"], 1)
                st.link(v.tensor_reduce(ts[0:n, :], ptop[0:n, 0:TOPK], AX.X, ALU.add))
                st.link(v.reciprocal(tr[0:n, :], ts[0:n, :]))
                st.link(v.tensor_scalar(wz[0:n, :], ptop[0:n, 0:TOPK], tr[0:n, :], None, ALU.mult))
                v.tensor_tensor(wdiag[0:n, 0:n, :], bass.AP(wz, 0, [[TOPK, n], [0, n], [1, TOPK]]),
                                bass.AP(ident, 0, [[128, n], [1, n], [0, TOPK]]), ALU.mult).then_inc(s["wdiag_done"], 1)

            def route_shares(g):
                b0, n = ROUTES[g]
                full(u, W_USE[g])
                v.tensor_copy(wbc[:, b0 * TOPK:(b0 + n) * TOPK], u.bank(W_USE[g])[:, 0:n * TOPK]).then_inc(s["route_done"], 1)
                dve.wait_ge(s["route_done"], g + 1)
                dve.sem_inc(s["misc_free"], 1)

            def hidden_free(g):
                dve.wait_ge(s["h_act"], g + 1)
                dve.sem_inc(s["misc_free"], 1)

            hidden_free(0)
            rt_copy(u, TAIL_R_USE)
            route_logits(0)
            o_scale(B - 1)
            route_top(0)
            residual(B - 1, u, TAIL_O_USE)
            route_shares(0)
            ln2_apply(B - 1)
            dve.wait_ge(s["setup_dve"], 1)

            def ffn_body(b, par):
                v.tensor_copy(wcur[:, par, :], wbc[:, bass.ds(b * TOPK, TOPK)]).then_inc(s["wcur_done"], 1)
                dve.wait_ge(s["wcur_done"], b + 1)
                for k in range(TOPK):
                    u = b * TOPK + k
                    for hf in range(2):
                        dve.wait_ge(s["hthi_done"], u * 2 + hf + 1)
                        v.scalar_tensor_tensor(out=hT[:, FT * SQ + hf * 448:FT * SQ + hf * 448 + 448], in0=bank[:, 2 + hf, 0:448],
                                               scalar=wcur[:, par, k:k + 1], in1=hT[:, hf * 448:hf * 448 + 448],
                                               op0=ALU.mult, op1=ALU.subtract).then_inc(s["htlo_done"], 1)
                    if isinstance(b, int) and b == 0:
                        if k == 0:
                            x2_lo(B - 1, uses(B - 1, 1), TAIL_X2_USE)
                        if k == 1:
                            hidden_free(1)
                            route_logits(1)
                            route_top(1)
                        if k == 2:
                            route_shares(1)
                dve.wait_ge(s["g2_done"], b * TOPK + TOPK)
                dve.wait_ge(s["r_loaded"], b * 16 + 16)
                if not (isinstance(b, int) and b == 0):
                    dve.wait_ge(s["out_written"], b * 16 - 15)
                v.scalar_tensor_tensor(out=ob[par], in0=bank[0:SQ, 4 + par, 0:D], scalar=tf_w[0:SQ, :], in1=rb[par],
                                       op0=ALU.mult, op1=ALU.add).then_inc(s["y_done"], 1)

            ffn_body(0, 0)
            with dve.Fori(0, (B - 2) // 2) as i:
                ffn_body(i * 2 + 1, 1)
                ffn_body(i * 2 + 2, 0)
            ffn_body(B - 1, 1)

        @block.tensor
        def _(pe):
            T = nc.tensor
            wq_s, wk_s, wv_s, wo_s = (wqkvo[:, n, :, :] for n in range(4))
            pe.wait_ge(s["ident_ready"], 1)

            def use(u, k, reads=-2):
                n = max(k - 2, reads)
                if not (isinstance(u.first, int) and u.n(n) <= 0):
                    pe.wait_ge(s["misc_free"], u.n(n))
                return u.bank(k)

            def full(ins):
                ins.then_inc(s["misc_full"], 1)

            def scores(b, par, p):
                if p == 0:
                    pe.wait_ge(s["k_stacked0"], b * 16 + 16)
                    pe.wait_ge(s["q_stacked"], b * 16 + 16)
                    pe.wait_ge(s["mask_ready"], b + 1)
                if not (isinstance(b, int) and b == 0 and p < 2):
                    pe.wait_ge(s["act_exp"], b * NH + 2 * p - 2)
                for e in range(2):
                    o = bank[0:SQ, 2 * (p % 2) + e, 0:SK]
                    T.matmul(o, ident_b[:, :], maskb[:, par, :], start=True, stop=False)
                    if e == 1 and p % (PAIRS // 2) == 0:
                        pe.wait_ge(s["k_stacked1" if p == 0 else "k_stacked2"], b * 16 + 16)
                    T.matmul(o, qst[64 * e:64 * e + 64, par, p, :], kst[64 * e:64 * e + 64, par, p * SK:(p + 1) * SK],
                             start=False, stop=True).then_inc(s["pe_s"], 1)

            def transpose_probs(b, p):
                for e in range(2):
                    pe.wait_ge(s["act_exp"], b * NH + 2 * p + e + 1)
                    for c in range(KC):
                        o = PTB + c * 256 + e * SQ
                        ins = T.transpose(flat[0:CK, o:o + SQ], probs[:, p % 2, e, c * CK:(c + 1) * CK], ident[0:SQ, 0:SQ])
                ins.then_inc(s["pe_t"], 1)

            def pv(b, p):
                t, j = p // 4, p % 4
                pe.wait_ge(s["act_pt"], b * PAIRS + p + 1)
                if p == 0:
                    pe.wait_ge(s["vpad_ready"], b + 1)
                    if not (isinstance(b, int) and b == 0):
                        pe.wait_ge(s["act_o"], b)
                o = flat[32 * j:32 * j + 32, PTB + 512 + OB + t * SQ:PTB + 512 + OB + (t + 1) * SQ]
                for e in range(2):
                    for c in range(KC):
                        ins = T.matmul(o, vpad[:, c, p, 32 * e:32 * e + 32], pT[:, p % 2, c, e * SQ:(e + 1) * SQ],
                                       start=(e == 0 and c == 0), stop=(e == 1 and c == KC - 1))
                ins.then_inc(s["pe_pv"], 1)

            def ctx_t(b, t, u, k):
                m = use(u, k)
                if t == 0:
                    pe.wait_ge(s["ctx_loaded"], b * 16 + 16)
                for c in range(KC):
                    ins = T.transpose(m[:, c * CK:(c + 1) * CK], ctx_s[:, c, t * 128:(t + 1) * 128], ident[0:CK, 0:CK])
                full(ins)

            def k_proj(t, u, k, ctx_use):
                m = use(u, k, ctx_use)
                for kt in range(DT):
                    ins = T.matmul(m[:, 0:SK], wk_s[:, kt, t * 128:(t + 1) * 128], ctxT[:, kt, :], start=(kt == 0), stop=(kt == DT - 1))
                full(ins)

            def x_t(b, u, k):
                pe.wait_ge(s["xn_done"], b + 1)
                m = use(u, k)
                for t in range(DT):
                    ins = T.transpose(m[:, t * SQ:(t + 1) * SQ], xa[:, t * 128:(t + 1) * 128], ident[0:SQ, 0:SQ])
                full(ins)

            def q_proj(u, k, x_use):
                m = use(u, k, x_use)
                for t in range(DT):
                    for kt in range(DT):
                        ins = T.matmul(m[:, t * SQ:(t + 1) * SQ], wq_s[:, kt, t * 128:(t + 1) * 128], xT[:, kt * SQ:(kt + 1) * SQ],
                                       start=(kt == 0), stop=(kt == DT - 1))
                full(ins)

            def v_proj(u):
                for k, cs in ((V_USE, (0, 1)), (V_USE + 1, (2,))):
                    m = use(u, k)
                    for c in cs:
                        for kt in range(DT):
                            ins = T.matmul(m[0:CK, (c % 2) * D:(c % 2 + 1) * D], ctxT[:, kt, c * CK:(c + 1) * CK], wv_s[:, kt, :],
                                           start=(kt == 0), stop=(kt == DT - 1))
                    full(ins)

            def r_t(b, u, k):
                pe.wait_ge(s["rexp_done"], b + 1)
                m = use(u, k)
                for t in range(DT):
                    ins = T.transpose(m[:, t * SQ:(t + 1) * SQ], rexp[:].rearrange("p h i -> p (h i)")[:, t * 128:(t + 1) * 128],
                                      ident[0:SQ, 0:SQ])
                full(ins)

            def o_proj(b, u, k):
                pe.wait_ge(s["dve_o"], b + 1)
                m = use(u, k)
                for t in range(DT):
                    ins = T.matmul(m[0:SQ, 0:D], oT[:, t * SQ:(t + 1) * SQ], wo_s[:, t, :], start=(t == 0), stop=(t == DT - 1))
                full(ins)

            def x2_t(b, u, k):
                pe.wait_ge(s["x2_done"], b + 1)
                m = use(u, k)
                for t in range(DT):
                    ins = T.transpose(m[:, t * SQ:(t + 1) * SQ], x2[:, t * 128:(t + 1) * 128], ident[0:SQ, 0:SQ])
                full(ins)

            prep_u = Uses(0, 0, shared)
            x_t(0, prep_u, 1)
            ctx_t(0, 0, prep_u, 2)
            ctx_t(0, 1, prep_u, 3)
            pe.wait_ge(s["wq_loaded"], 16)
            q_proj(prep_u, 4, 1)
            pe.wait_ge(s["wk_loaded"], 16)
            k_proj(0, prep_u, 5, 3)
            k_proj(1, prep_u, 6, 3)
            pe.wait_ge(s["wv_loaded"], 16)
            v_proj(uses(0, 0))
            pe.wait_ge(s["setup_pool"], 1)
            scores(0, 0, 0)
            scores(0, 0, 1)

            def body(b, par):
                first = isinstance(b, int) and b == 0
                last = isinstance(b, int) and b == B - 1
                u = uses(b, par)
                for p in range(PAIRS):
                    if p > 0:
                        pv(b, p - 1)
                    elif not first:
                        r_t(b - 1, u, R_USE)
                        pv(b - 1, PAIRS - 1)
                    transpose_probs(b, p)
                    if not last:
                        if p == 1:
                            x_t(b + 1, u, X_USE)
                            ctx_t(b + 1, 0, u, CTX_USE)
                        if p == 2:
                            k_proj(0, u, K_USE, CTX_USE + 1)
                            k_proj(1, u, K_USE + 1, CTX_USE + 1)
                    if p == 0 and not first:
                        v_proj(u)
                    if p < PAIRS - 2:
                        scores(b, par, p + 2)
                    elif not last:
                        scores(b + 1, 1 - par, p - PAIRS + 2)
                    if not last:
                        if p == 1:
                            ctx_t(b + 1, 1, u, CTX_USE + 1)
                            q_proj(u, Q_USE, X_USE)
                    if p == 3 and not first:
                        o_proj(b - 1, u, LAST_O_USE if last else O_USE)
                    if p == 6 and not first:
                        x2_t(b - 1, u, LAST_X2_USE if last else X2_USE)
                if first:
                    pe.wait_ge(s["wo_loaded"], DT * 4 * 16)

            over_batches(pe, body)
            u = uses(B - 1, 1)

            def route_h(g):
                b0, n = ROUTES[g]
                m = use(u, H_USE[g], LAST_X2_USE if g == 0 else TAIL_X2_USE)
                for t in range(DT):
                    ins = T.matmul(m[0:RH, 0:n], w1_s[:, t, :], pooled[:, t, b0:b0 + n], start=(t == 0), stop=(t == DT - 1))
                full(ins)

            def route_l(g):
                n = ROUTES[g][1]
                m = use(u, L_USE[g])
                pe.wait_ge(s["h_act"], g + 1)
                full(T.matmul(m[0:n, 0:NZ], h_s[:, 0:n], w2_s[:, :], start=True, stop=True))

            def route_w(g):
                n = ROUTES[g][1]
                m = use(u, W_USE[g])
                pe.wait_ge(s["wdiag_done"], g + 1)
                full(T.matmul(m[:, 0:n * TOPK], ones[0:n, :], wdiag[0:n, :, :].rearrange("p a b -> p (a b)")[:, 0:n * TOPK],
                              start=True, stop=True))

            pe.wait_ge(s["const_loaded"], 80)
            route_h(0)
            r_t(B - 1, u, TAIL_R_USE)
            pv(B - 1, PAIRS - 1)
            route_l(0)
            o_proj(B - 1, u, TAIL_O_USE)
            route_w(0)
            pe.wait_ge(s["idx_loaded"], 16)
            pe.wait_ge(s["hi_done"], NCH)
            pe.wait_ge(s["lo_done"], NCH)

            def zone(b, k):
                return pe.value_load(idx_row[0:1, bass.ds(b * NZ + k, 1)], min_val=0, max_val=NZ - 1)

            def g1(b, par, k, e, hf):
                u = b * TOPK + k
                if k == 0 and hf == 0:
                    pe.wait_ge(s["x2b_loaded"], b * 16 + 16)
                if not (isinstance(u, int) and u == 0):
                    pe.wait_ge(s["gelu_done"], u * 2 - 1 + hf)
                o = bank[0:SQ, hf, :]
                n = 0
                for t in range(DT):
                    for xs, ws in ((0, 0), (0, 1), (1, 0)):
                        ins = T.matmul(o, x2b[:, par, xs * DT * SQ + t * SQ:xs * DT * SQ + (t + 1) * SQ],
                                       wa[:, bass.ds(e * (4 * CHUNK) + ws * (2 * CHUNK) + t * CHUNK + hf * 512, 512)],
                                       start=(n == 0), stop=(n == 3 * DT - 1))
                        n += 1
                ins.then_inc(s["g1_done"], 1)

            def ht(b, k, hf):
                u = b * TOPK + k
                pe.wait_ge(s["gelu_done"], u * 2 + hf + 1)
                if not (isinstance(u, int) and u == 0):
                    pe.wait_ge(s["htlo_done"], u * 2 - 1 + hf)
                for f in range(4):
                    ins = T.transpose(bank[:, 2 + hf, f * SQ:(f + 1) * SQ], h_f[:, hf * 512 + f * 128:hf * 512 + (f + 1) * 128],
                                      ident[0:SQ, 0:SQ])
                ins.then_inc(s["ht_full"], 1)

            def g2(b, par, k, e):
                u = b * TOPK + k
                if k == 0 and not (isinstance(b, int) and b < 2):
                    pe.wait_ge(s["y_done"], b)
                o = bank[0:SQ, 4 + par, 0:D]
                for f in range(FT):
                    if f % 4 == 0:
                        pe.wait_ge(s["htlo_done"], u * 2 + f // 4 + 1)
                    for hs, ws in ((0, 0), (0, 1), (1, 0)):
                        ins = T.matmul(o, hT[:, hs * FT * SQ + f * SQ:hs * FT * SQ + (f + 1) * SQ],
                                       wb[:, bass.ds(e * (4 * CHUNK) + ws * (2 * CHUNK) + f * D, D)],
                                       start=(k == 0 and f == 0 and hs == 0 and ws == 0), stop=(k == TOPK - 1 and f == FT - 1 and hs == 1))
                ins.then_inc(s["g2_done"], 1)

            def ffn_body(b, par, last):
                e = None
                for k in range(TOPK):
                    if k < TOPK - 1:
                        nxt = (b, par, k + 1, zone(b, k + 1))
                    elif not last:
                        if not (isinstance(b, int) and b == 0):
                            pe.wait_ge(s["idx_loaded"], 32)
                        nxt = (b + 1, 1 - par, 0, zone(b + 1, 0))
                    else:
                        nxt = None
                    if isinstance(b, int) and b == 0 and k == 1:
                        route_h(1)
                    ht(b, k, 0)
                    if nxt:
                        g1(*nxt, 0)
                    ht(b, k, 1)
                    if nxt:
                        g1(*nxt, 1)
                    if e is None:
                        e = zone(b, k)
                    if isinstance(b, int) and b == 0:
                        if k == 0:
                            x2_t(B - 1, u, TAIL_X2_USE)
                        if k == 1:
                            route_l(1)
                        if k == 2:
                            route_w(1)
                    g2(b, par, k, e)
                    e = nxt[3] if nxt else None

            e0 = zone(0, 0)
            g1(0, 0, 0, e0, 0)
            g1(0, 0, 0, e0, 1)
            ffn_body(0, 0, False)
            with pe.Fori(0, (B - 2) // 2) as i:
                ffn_body(i * 2 + 1, 1, False)
                ffn_body(i * 2 + 2, 0, False)
            ffn_body(B - 1, 1, True)


_INS = ["x", "ctx_1024", "mask_Bx1xSxS2_bk1", "g_xattn", "g_ffn", "L0_xattn_Wq", "L0_xattn_bq", "L0_xattn_Wk", "L0_xattn_bk",
        "L0_xattn_Wv", "L0_xattn_bv", "L0_xattn_Wo", "L0_xattn_bo", "L0_ffn_W1", "L0_ffn_b1", "L0_ffn_W2", "L0_ffn_b2",
        "L0_ffn_Wa", "L0_ffn_Wb"]


def kernel(**inputs):
    import numpy as np
    import concourse.bacc as bacc
    from concourse.bass_utils import run_bass_kernel_spmd as run

    nc = bacc.Bacc("TRN2", target_bir_lowering=False, num_devices=1)
    arrays, args = {}, []
    for name in _INS:
        a = np.ascontiguousarray(inputs[name])
        if a.dtype == np.bool_:
            a = a.reshape(B, SQ, SK)
        arrays[f"in_{name}"] = a
        args.append(nc.dram_tensor(f"in_{name}", a.shape, mybir.dt.from_np(a.dtype), kind="ExternalInput").ap())
    args.append(nc.dram_tensor("out_0", (B, SQ, D), F32, kind="ExternalOutput").ap())
    flamingo_layer(nc, *args)
    r = run(nc, [arrays], core_ids=[0])
    return r.results[0]["out_0"]
```
